# Optimizing a Trainium2 kernel written in Bass

```python
import numpy as np
import jax
import jax.numpy as jnp

def _softmax(x, axis=-1):
    return jax.nn.softmax(x, axis=axis)

def _gelu(x):
    return jax.nn.gelu(x, approximate=True)

def _silu(x):
    return jax.nn.silu(x)

def _sigmoid(x):
    return jax.nn.sigmoid(x)

def _layernorm(x, axis=-1, eps=1e-05):
    m = jnp.mean(x, axis=axis, keepdims=True)
    v = jnp.var(x, axis=axis, keepdims=True)
    return (x - m) / jnp.sqrt(v + eps)

def _scatter_add(tgt, idx, src, axis=0):
    return tgt.at[idx].add(src)

def _segment_sum(src, seg, n):
    return jax.ops.segment_sum(src, seg, n)
kernel_name = 'mk_seq_preln_d1_jaxref_r4_5ad24f'

def setup_inputs(seed: int=0):
    np.random.seed(seed)
    _w = jnp.asarray

    def _L0_attn_setup():
        import jax, jax.numpy as jnp
        import numpy as np
        EMB = 256
        HEADS = 16
        key = jax.random.key(seed)
        ks = jax.random.split(key, 6)
        s = 1.0 / np.sqrt(EMB)
        x = jax.random.normal(ks[0], (2, 512, EMB), dtype=jnp.float32)
        Wk = jax.random.normal(ks[1], (EMB, EMB), dtype=jnp.float32) * s
        Wq = jax.random.normal(ks[2], (EMB, EMB), dtype=jnp.float32) * s
        Wv = jax.random.normal(ks[3], (EMB, EMB), dtype=jnp.float32) * s
        Wo = jax.random.normal(ks[4], (EMB, EMB), dtype=jnp.float32) * s
        bo = jax.random.normal(ks[5], (EMB,), dtype=jnp.float32) * s
        return {'x': x, 'Wk': Wk, 'Wq': Wq, 'Wv': Wv, 'Wo': Wo, 'bo': bo}
    _L0_attn_in = _L0_attn_setup()

    def _L0_ffn_setup():
        import jax, jax.numpy as jnp
        import numpy as np
        B, T, D = (4, 512, 256)
        H, DH, E, SEL = (8, 64, 5, 2)

        def _topk_mask(logits, k):
            _, idx = jax.lax.top_k(logits, k)
            return jnp.sum(jax.nn.one_hot(idx, logits.shape[-1], dtype=logits.dtype), axis=-2)
        key = jax.random.key(seed)
        ks = jax.random.split(key, 7)
        s = 0.02
        x = jax.random.normal(ks[0], (B, T, D), dtype=jnp.float32)
        Wq = jax.random.normal(ks[1], (D, H * DH), dtype=jnp.float32) * s
        Wk = jax.random.normal(ks[2], (D, H * DH), dtype=jnp.float32) * s
        Ws = jax.random.normal(ks[3], (D, H * E), dtype=jnp.float32) * s
        Wd = jax.random.normal(ks[4], (D, H * E), dtype=jnp.float32) * s
        Wv = jax.random.normal(ks[5], (E, D, DH), dtype=jnp.float32) * s
        Wo = jax.random.normal(ks[6], (E, DH, D), dtype=jnp.float32) * s
        return {'x': x, 'Wq': Wq, 'Wk': Wk, 'Ws': Ws, 'Wd': Wd, 'Wv': Wv, 'Wo': Wo}
    _L0_ffn_in = _L0_ffn_setup()
    _d = {'L0_attn_x': _L0_attn_in['x'], 'L0_attn_Wk': _L0_attn_in['Wk'], 'L0_attn_Wq': _L0_attn_in['Wq'], 'L0_attn_Wv': _L0_attn_in['Wv'], 'L0_attn_Wo': _L0_attn_in['Wo'], 'L0_attn_bo': _L0_attn_in['bo'], 'L0_ffn_Wq': _L0_ffn_in['Wq'], 'L0_ffn_Wk': _L0_ffn_in['Wk'], 'L0_ffn_Ws': _L0_ffn_in['Ws'], 'L0_ffn_Wd': _L0_ffn_in['Wd'], 'L0_ffn_Wv': _L0_ffn_in['Wv'], 'L0_ffn_Wo': _L0_ffn_in['Wo']}
    _x0 = _d['L0_attn_x']
    _d['L0_attn_x'] = jax.random.normal(jax.random.fold_in(jax.random.key(seed), 1), (32, 512, 256), dtype=_x0.dtype)
    del _x0
    return _d

def reference(L0_attn_x, L0_attn_Wk, L0_attn_Wq, L0_attn_Wv, L0_attn_Wo, L0_attn_bo, L0_ffn_Wq, L0_ffn_Wk, L0_ffn_Ws, L0_ffn_Wd, L0_ffn_Wv, L0_ffn_Wo):

    def _L0_attn_ref(x, Wk, Wq, Wv, Wo, bo):
        import jax, jax.numpy as jnp
        import numpy as np
        EMB = 256
        HEADS = 16
        b, seq, emb = x.shape
        h = HEADS
        hd = emb // h
        k = (x @ Wk.T).reshape(b, seq, h, hd).transpose(0, 2, 1, 3)
        q = (x @ Wq.T).reshape(b, seq, h, hd).transpose(0, 2, 1, 3)
        v = (x @ Wv.T).reshape(b, seq, h, hd).transpose(0, 2, 1, 3)
        scores = jnp.einsum('bhqd,bhkd->bhqk', q, k) / jnp.sqrt(jnp.float32(emb))
        attn = jax.nn.softmax(scores, axis=-1)
        out = jnp.einsum('bhqk,bhkd->bhqd', attn, v)
        out = out.transpose(0, 2, 1, 3).reshape(b, seq, emb)
        return out @ Wo.T + bo

    def _L0_ffn_ref(x, Wq, Wk, Ws, Wd, Wv, Wo):
        import jax, jax.numpy as jnp
        import numpy as np
        B, T, D = (4, 512, 256)
        H, DH, E, SEL = (8, 64, 5, 2)

        def _topk_mask(logits, k):
            _, idx = jax.lax.top_k(logits, k)
            return jnp.sum(jax.nn.one_hot(idx, logits.shape[-1], dtype=logits.dtype), axis=-2)
        e, d, dh = Wv.shape
        h = Wq.shape[1] // dh
        b, t, _ = x.shape
        scale = dh ** (-0.5)
        q = (x @ Wq).reshape(b, t, h, dh).transpose(0, 2, 1, 3)
        k = (x @ Wk).reshape(b, t, h, dh).transpose(0, 2, 1, 3)
        gl_v = (x @ Ws).reshape(b, t, h, e)
        wv = _topk_mask(gl_v, SEL) * jax.nn.sigmoid(gl_v)
        xv = jnp.einsum('btd,edk->btek', x, Wv)
        v = jnp.einsum('bthe,btek->bhtk', wv, xv)
        scores = jnp.einsum('bhid,bhjd->bhij', q * scale, k)
        probs = jax.nn.softmax(scores, axis=-1)
        attn = jnp.einsum('bhij,bhjd->bihd', probs, v)
        gl_o = (x @ Wd).reshape(b, t, h, e)
        mask_o = _topk_mask(gl_o, SEL)
        out = jnp.einsum('bthe,bthk,ekd->btd', mask_o, attn, Wo)
        return out
    x = L0_attn_x
    x = x + _L0_attn_ref(_layernorm(x, axis=-1), L0_attn_Wk, L0_attn_Wq, L0_attn_Wv, L0_attn_Wo, L0_attn_bo)
    x = x + _L0_ffn_ref(_layernorm(x, axis=-1), L0_ffn_Wq, L0_ffn_Wk, L0_ffn_Ws, L0_ffn_Wd, L0_ffn_Wv, L0_ffn_Wo)
    return x

_drawn_inputs = setup_inputs


def setup_inputs(seed=0):
    import zlib

    import numpy as np

    out = dict(_drawn_inputs(seed))
    spreads = {}
    factors = {'L0_attn_Wk': 2.908,
     'L0_attn_Wq': 2.859,
     'L0_ffn_Wq': 8.0,
     'L0_ffn_Wk': 8.0,
     'L0_ffn_Ws': 6.204,
     'L0_ffn_Wd': 5.668,
     'L0_ffn_Wv': 2.857,
     'L0_ffn_Wo': 2.765}
    for name, (base, spread) in spreads.items():
        noise = np.random.default_rng([zlib.crc32(name.encode()), seed]).standard_normal(out[name].shape)
        drawn = base * np.exp(spread * noise) if base else spread * noise
        out[name] = jnp.asarray(drawn.astype(out[name].dtype))
    for name, factor in factors.items():
        out[name] = (out[name] * factor).astype(out[name].dtype)
    return out
```

```python
from contextlib import ExitStack

import numpy as np
import concourse.bass as bass
from concourse import mybir

NB, T, D = 32, 512, 256
ENGINES = ("sync", "tensor", "scalar", "vector", "gpsimd")


class Step:

    def __init__(self, eng, deps, fn, cost, dma):
        self.eng, self.deps, self.fn, self.cost, self.dma = eng, deps, fn, cost, dma
        self.used = False
        self.end = None
        self.sem = self.value = None


class Queues:

    def __init__(self):
        self.threads = {}
        self.order = {e: [] for e in ENGINES}

    def add(self, thread, eng, fn, deps, cost, dma=None):
        deps = [d for d in deps if d is not None]
        s = Step(eng, deps, fn, cost, dma)
        for d in deps:
            d.used = True
        self.threads.setdefault((eng, thread), []).append(s)
        return s

    def settle(self):
        free = {e: 0.0 for e in ENGINES}
        head = {k: 0 for k in self.threads}
        live = {e: [k for k in self.threads if k[0] == e] for e in ENGINES}
        while True:
            best = None
            for e in ENGINES:
                for k in live[e]:
                    q = self.threads[k]
                    if head[k] >= len(q):
                        continue
                    s = q[head[k]]
                    at = free[e]
                    ok = True
                    for d in s.deps:
                        if d.end is None:
                            ok = False
                            break
                        at = max(at, d.end + 0.08)
                    if ok and (best is None or at < best[0]):
                        best = (at, k, s)
            if best is None:
                break
            at, k, s = best
            head[k] += 1
            hold = 0.06 if s.dma is not None else s.cost
            free[k[0]] = at + hold
            s.end = at + s.cost + (0 if k[0] != "tensor" else 0.1)
            self.order[k[0]].append(s)
        assert all(head[k] == len(q) for k, q in self.threads.items()), "queues are stuck"


def program(nc, t):
    F32, BF, F32R = mybir.dt.float32, mybir.dt.bfloat16, mybir.dt.float32r
    ALU, ACT, AX = mybir.AluOpType, mybir.ActivationFunctionType, mybir.AxisListType
    ctx = ExitStack()
    Q = Queues()
    with ctx:
        def sb(name, shape, dt=F32):
            return ctx.enter_context(nc.sbuf_tensor("s_" + name, shape, dt))

        def sem(name):
            return ctx.enter_context(nc.semaphore("m_" + name))

        def dram(name, shape, dt):
            return nc.dram_tensor("w_" + name, shape, dt, kind="Internal").ap()

        ident = sb("ident", [128, 128])
        wq = sb("wq", [128, 2, 256])
        wk = sb("wk", [128, 2, 256])
        wv = sb("wv", [128, 2, 256])
        wo = sb("wo", [128, 2, 256])
        bo = sb("bo", [128, 256])
        fq = sb("fq", [128, 2, 512])
        fk = sb("fk", [128, 2, 512])
        fg = sb("fg", [128, 2, 400])
        fo = sb("fo", [128, 3, 256])
        nhalf = sb("nhalf", [128, 4])
        xa = sb("xa", [128, 3, 4, 256])
        xt = sb("xt", [128, 2, 512])
        sta = sb("sta", [128, 4, 6])
        mva = sb("mva", [128, 4, 2])
        vea = sb("vea", [128, 4])
        rsa = sb("rsa", [128, 4])
        pt = sb("pt", [128, 2, 3, 512], BF)
        res = sb("res", [128, 2, 512])
        qs = sb("qs", [128, 2, 8, 512], BF)
        ks = sb("ks", [128, 2, 8, 512], BF)
        v32 = sb("v32", [128, 4, 16, 32])
        mxa = sb("mxa", [128, 2, 4, 8])
        mp = sb("mp", [8, 1, 3, 512], BF)
        mr = res[0:8, 1, :]
        pa = sb("pa", [128, 2, 4, 512])
        t1 = sb("t1", [128, 2, 512])
        xn = t1[:, :, :].rearrange("p a (i n) -> p (a i) n", i=2)
        rca = sb("rca", [128, 2, 16])
        comb = res[:, 0, :]
        ont = sb("ont", [128, 2, 512])
        stf = sb("stf", [128, 4, 6])
        mvf = sb("mvf", [128, 4, 2])
        vef = sb("vef", [128, 4])
        rsf = sb("rsf", [128, 4])
        tmp = sb("tmp", [128, 2048])
        xf = sb("xf", [128, 2, 512])
        xg = sb("xg", [128, 4, 400])
        cmpt = sb("cmpt", [128, 64, 5, 5], BF)
        rank = sb("rank", [128, 64, 5])
        mask = sb("mask", [128, 4, 2, 8, 5])
        sg = sb("sg", [128, 4, 8, 5])
        sg2 = sb("sg2", [128, 4, 8, 5])
        wvx = sb("wvx", [128, 4, 8, 5])
        v65 = sb("v65", [128, 4, 8, 65])
        q1 = sb("q1", [128, 4, 512], F32R)
        q2 = sb("q2", [128, 4, 512], F32R)
        k1 = sb("k1", [128, 4, 512], F32R)
        k2 = sb("k2", [128, 4, 512], F32R)
        mxf = sb("mxf", [128, 4, 4])
        mfh = sb("mfh", [4, 2, 512], F32R)
        pf = sb("pf", [128, 3, 512])
        osb = sb("osb", [65, 512])
        rcf = sb("rcf", [128, 2, 4])
        w2 = sb("w2", [128, 2, 4, 5])
        pu = sb("pu", [128, 4, 320])
        uu = sb("uu", [128, 4, 320])
        ut = tmp[:, 0:1536].rearrange("p (k n) -> p k n", k=3)

        bank = [ctx.enter_context(nc.psum_tensor(f"bank{i}", [128, 512], F32)) for i in range(8)]

        parts = dram("parts", [2, 2, 2, 3, 128, 512], BF)
        maxa = dram("maxa", [2, 2, 3, 8, 512], BF)
        maxf = dram("maxf", [2, 2, 2, 4, 512], F32)

        dma_sems, dma_counts = {}, {}

        def op(thread, eng, fn, deps=(), cost=0.3):
            return Q.add(thread, eng, fn, list(deps), cost)

        def pe(th, fn, deps=(), cost=0.22):
            return op(th, "tensor", fn, deps, cost)

        def act(th, fn, deps=(), cost=0.6):
            return op(th, "scalar", fn, deps, cost)

        def dve(th, fn, deps=(), cost=0.65):
            return op(th, "vector", fn, deps, cost)

        def pool(th, fn, deps=(), cost=1.0):
            return op(th, "gpsimd", fn, deps, cost)

        def dma(th, site, dst, src, deps=(), cost=2.5):
            if site not in dma_sems:
                dma_sems[site] = sem("d_" + site)
                dma_counts[site] = [0, None]
            last = dma_counts[site][1]
            s = Q.add(th, "sync", lambda e: e.dma_start(dst, src), list(deps) + [last], cost, dma=site)
            dma_counts[site][0] += 16
            dma_counts[site][1] = s
            s.sem, s.value = dma_sems[site], dma_counts[site][0]
            return s

        class Ring:

            def __init__(self, banks):
                self.banks, self.readers, self.n = banks, [[] for _ in banks], -1

            def take(self):
                self.n = (self.n + 1) % len(self.banks)
                return self.banks[self.n], self.readers[self.n], self.n

            def read_by(self, n, *steps):
                self.readers[n] = list(steps)

        ra, rf = Ring(bank[0:3]), Ring(bank[3:6])
        oa, of = bank[6], bank[7]

        loads = []
        for name, dst, src in [
            ("ident", ident[:, :], t["ident"]),
            ("wq", wq[:, :, :], t["wq"].rearrange("(c p) n -> p c n", p=128)),
            ("wk", wk[:, :, :], t["wk"].rearrange("(c p) n -> p c n", p=128)),
            ("wv", wv[:, :, :], t["wv"].rearrange("(c p) n -> p c n", p=128)),
            ("wo", wo[:, :, :], t["wo"].rearrange("(c p) n -> p c n", p=128)),
            ("bo", bo[:, :], t["bo"]),
            ("fq", fq[:, :, :], t["fq"].rearrange("(c p) n -> p c n", p=128)),
            ("fk", fk[:, :, :], t["fk"].rearrange("(c p) n -> p c n", p=128)),
            ("fg", fg[:, :, :], t["fg"].rearrange("(c p) n -> p c n", p=128)),
            ("fo", fo[:, 0:2, :], t["fo"][0:256, :].rearrange("(c p) n -> p c n", p=128)),
            ("fo2", fo[0:64, 2, :], t["fo"][256:320, :]),
        ]:
            loads.append(dma("load", name, dst, src))
        L = dict(zip(["ident", "wq", "wk", "wv", "wo", "bo", "fq", "fk", "fg", "fo", "fo2"], loads))
        c_half = pool("a", lambda e: e.memset(nhalf[:, :], -0.5))
        c_v32 = pool("a", lambda e: e.memset(v32[:, :, :, 16:32], 1.0))
        c_ks = dve("a", lambda e: e.memset(ks[96:99, :, :, :], 1.0), cost=8)
        c_v65 = pool("a", lambda e: e.memset(v65[:, :, :, 64:65], 1.0))
        c_k2z = dve("a", lambda e: e.memset(k2[64:128, :, :].bitcast(F32), 0.0))
        c_k2o = dve("a", lambda e: e.memset(k2[64:66, :, :].bitcast(F32), 1.0), [c_k2z])
        c_q2z = dve("a", lambda e: e.memset(q2[64:128, :, :].bitcast(F32), 0.0))
        c_cmp = dve("a", lambda e: e.memset(cmpt[:, :, :, :], 0.0))

        def layernorm(th, x, st, mv, ve, rs, out, ready, free):
            a = [dve(th, lambda e, i=i: e.bn_stats(st[:, i, :], x[:, i, :]), [ready], 0.35) for i in range(4)]
            g = [dve(th, lambda e, i=i: e.bn_aggr(mv[:, i, :], st[:, i, :]), [a[i]], 0.12) for i in range(4)]
            v = dve(th, lambda e: e.tensor_scalar_add(ve[:, :], mv[:, :, 1], 1e-5), [g[3]], 0.1)
            r = pool(th, lambda e: e.tensor_tensor(rs[:, :], ve[:, :], nhalf[:, :], ALU.pow), [v, c_half], 0.2)
            return [dve(th, lambda e, i=i: e.tensor_scalar(out[:, i, :], x[:, i, :], mv[:, i, 0:1], rs[:, i:i + 1],
                                                          ALU.subtract, ALU.mult), [r] + free, 0.25)
                    for i in range(4)]

        def transposed(th, ring, src, dst, ready, free):
            out = []
            for f in range(2):
                b, busy, n = ring.take()

                def go(e, b=b, f=f):
                    for i in range(4):
                        r = e.transpose(b[:, 128 * i:128 * i + 128], src[:, i, 128 * f:128 * f + 128], ident[:, :])
                    return r
                p = pe(th, go, busy + ready + [L["ident"]], 0.5)
                c = act(th, lambda e, b=b, f=f: e.copy(dst[:, f, :], b[:, :]), [p] + free)
                ring.read_by(n, c)
                out.append((p, c))
            return [p for p, _ in out], [c for _, c in out]

        def attn(b, S):
            A, X = b % 2, b % 3
            x = xa[:, X, :, :]
            ld = dma("ld", f"x{X}", x, t["x"][b].rearrange("(c p) n -> p c n", p=128), [S["xfree"][X]])
            nrm = layernorm("a", x, sta, mva, vea, rsa, xn, ld, [S["xn_free"]] + S["t1"])
            xb = [pool("a", lambda e, i=i: e.tensor_tensor(x[:, i, :], x[:, i, :], bo[:, :], ALU.add),
                       [nrm[3], L["bo"]], 0.6) for i in range(4)]
            tp, tc_ = transposed("a", ra, xn, xt, [nrm[3]], [S["xt_free"]])
            S["xn_free"] = tp[1]
            stacked = {}
            last_proj = None
            for c in range(2):
                for z, (w, lw, dst) in enumerate(((wq, "wq", qs), (wk, "wk", ks))):
                    bk, busy, n = ra.take()
                    u = z
                    P3 = pt[:, u, :, :]

                    def go(e, bk=bk, w=w, c=c):
                        for f in range(2):
                            r = e.matmul(bk[:, :], w[:, f, 128 * c:128 * c + 128], xt[:, f, :],
                                         start=(f == 0), stop=(f == 1))
                        return r
                    p = pe("a", go, busy + tc_ + [L[lw]], 1.72)
                    last_proj = p
                    hi = act("a", lambda e, bk=bk, P3=P3: e.copy(P3[:, 0, :], bk[:, :]), [p, S["pt"][u]])
                    r1 = dve("a", lambda e, bk=bk, P3=P3, u=u: e.tensor_tensor(res[:, u, :], bk[:, :], P3[:, 0, :],
                                                                         ALU.subtract), [hi, S["res"][u]])
                    ra.read_by(n, r1)
                    mid = pool("a", lambda e, P3=P3, u=u: e.tensor_copy(P3[:, 1, :], res[:, u, :]), [r1], 0.8)
                    lo = pool("a", lambda e, P3=P3, u=u: e.tensor_tensor(P3[:, 2, :], res[:, u, :], P3[:, 1, :],
                                                                   ALU.subtract), [mid], 1.2)
                    S["res"][u] = lo
                    st = dma("a", f"pw{z}{c}", parts[A, z, c].rearrange("s p n -> p s n"), P3, [lo, S["parts"][A, z, c]])
                    S["pt"][u] = st
                    sd = parts[A, z, c].rearrange("s (d h) n -> (s d) h n", h=8)
                    cuts = [(0, 0, 48), (48, 0, 32), (80, 0, 16)] if z == 0 else \
                        [(0, 0, 16), (16, 0, 16), (32, 0, 16), (48, 16, 16), (64, 16, 16), (80, 32, 16)]
                    got = []
                    for j, (to, fr, k) in enumerate(cuts):
                        got.append(dma("a", f"pr{z}{c}{j}", dst[to:to + k, c, :, :], sd[fr:fr + k, :, :],
                                       [st, S["stack"][c]]))
                    stacked[z, c] = got
                    S["parts"][A, z, c] = got[-1]
            vd = []
            for i2 in range(2):
                bk, busy, n = ra.take()

                def go(e, bk=bk, i2=i2):
                    for i in range(2):
                        for f in range(2):
                            tc = 2 * i2 + i
                            r = e.matmul(bk[:, 256 * i:256 * i + 256], xt[:, f, 128 * tc:128 * tc + 128], wv[:, f, :],
                                         start=(f == 0), stop=(f == 1))
                    return r
                p = pe("a", go, busy + tc_ + [L["wv"]], 1.74)
                last_proj = p
                c_ = act("a", lambda e, bk=bk, i2=i2: e.copy(
                    v32[:, 2 * i2:2 * i2 + 2, :, 0:16], bk[:, :].rearrange("p (i h d) -> p i h d", i=2, h=16)),
                    [p, c_v32, S["v32"]])
                ra.read_by(n, c_)
                vd.append(c_)
            S["xt_free"] = last_proj
            rows = []
            for c in range(2):
                mx = None
                for h in range(8):
                    for i in range(4):
                        bk, busy, n = ra.take()
                        p = pe("a", lambda e, bk=bk, c=c, h=h, i=i: e.matmul(
                            bk[:, :], qs[0:96, c, h, 128 * i:128 * i + 128], ks[0:96, c, h, :], start=True, stop=True),
                            busy + stacked[0, c] + stacked[1, c])
                        mx = dve("a", lambda e, bk=bk, c=c, h=h, i=i: e.tensor_reduce(
                            mxa[:, c, i, h:h + 1], bk[:, :], AX.X, ALU.max, negate=True), [p, S["mxa"][c]])
                        ra.read_by(n, mx)
                bk, busy, n = ra.take()

                def go(e, bk=bk, c=c):
                    for i in range(4):
                        r = e.transpose(bk[0:8, 128 * i:128 * i + 128], mxa[:, c, i, :], ident[:, :])
                    return r
                p = pe("a", go, busy + [mx], 0.4)
                S["mxa"][c] = p
                h1 = act("a", lambda e, bk=bk, c=c: e.copy(mp[:, 0, 0, :], bk[0:8, :]), [p, S["mp"]])
                r1 = dve("a", lambda e, bk=bk, c=c: e.tensor_tensor(mr, bk[0:8, :], mp[:, 0, 0, :],
                                                                    ALU.subtract), [h1, S["res"][1]])
                ra.read_by(n, r1)
                m1 = dve("a", lambda e, c=c: e.tensor_copy(mp[:, 0, 1, :], mr), [r1], 0.35)
                l1 = dve("a", lambda e, c=c: e.tensor_tensor(mp[:, 0, 2, :], mr, mp[:, 0, 1, :],
                                                             ALU.subtract), [m1])
                S["res"][1] = l1
                w = dma("a", f"mw{c}", maxa[A, c].rearrange("s h n -> h s n"), mp[:, 0, :, :], [l1, S["maxa"][A, c]])
                S["mp"] = w
                g = dma("a", f"mr{c}", qs[96:99, c, :, :], maxa[A, c], [w, S["stack"][c]])
                S["maxa"][A, c] = g
                rows.append(g)
            outs = []
            for j in range(4):
                c = j // 2
                pv = None
                for kc in range(4):
                    slot = kc % 2
                    ex = []
                    for g in range(4):
                        h = 4 * (j % 2) + g
                        bk, busy, n = ra.take()
                        p = pe("a", lambda e, bk=bk, c=c, h=h, kc=kc: e.matmul(
                            bk[:, :], ks[0:99, c, h, 128 * kc:128 * kc + 128], qs[0:99, c, h, :],
                            start=True, stop=True), busy + [rows[c], c_ks])
                        x_ = act("a", lambda e, bk=bk, slot=slot, g=g: e.activation(
                            pa[:, slot, g, :], bk[:, :], ACT.Exp, scale=0.0625), [p, S["pa"][slot]])
                        ra.read_by(n, x_)
                        ex.append(x_)

                    def go(e, slot=slot, kc=kc, j=j):
                        for g in range(4):
                            r = e.matmul(oa[32 * g:32 * g + 32, :], v32[:, kc, 4 * j + g, :], pa[:, slot, g, :],
                                         start=(kc == 0), stop=(kc == 3))
                        return r
                    pv = pe("apv", go, ex + vd + ([S["oa"]] if kc == 0 else []), 0.9)
                    S["pa"][slot] = pv
                if j % 2:
                    S["stack"][c] = p
                B, a = j % 2, j % 2
                tr = dve("apv", lambda e, B=B: e.transpose(t1[:, B, :], oa[:, :]), [pv, S["t1"][B], S["xn_free"]])
                S["oa"] = tr
                t4 = t1[:, B, :].rearrange("p (k j) -> p k j", j=32)
                rc = dve("apv", lambda e, B=B, t4=t4: e.reciprocal(rca[:, B, :], t4[:, :, 16]), [tr], 0.15)
                ml = dve("apv", lambda e, B=B, t4=t4, a=a: e.tensor_tensor(
                    comb.rearrange("p (k j) -> p k j", j=32)[:, :, 16 * a:16 * a + 16], t4[:, :, 0:16],
                    rca[:, B, :].unsqueeze(2).to_broadcast([128, 16, 16]), ALU.mult), [rc, S["comb"], S["res"][0]], 0.35)
                S["t1"][B] = ml
                if a:
                    tt = dve("apv", lambda e, j=j: e.transpose(ont[:, j // 2, :], comb),
                             [ml, S["ont"]])
                    S["comb"] = S["res"][0] = tt
                    outs.append(tt)
            S["v32"] = pv
            done = []
            for i2 in range(2):
                bk, busy, n = ra.take()

                def go(e, bk=bk, i2=i2):
                    for i in range(2):
                        for f in range(2):
                            tc = 2 * i2 + i
                            r = e.matmul(bk[:, 256 * i:256 * i + 256], ont[:, f, 128 * tc:128 * tc + 128], wo[:, f, :],
                                         start=(f == 0), stop=(f == 1))
                    return r
                p = pe("a", go, busy + outs + [L["wo"]], 1.74)
                s = dve("a", lambda e, bk=bk, i2=i2, A=A: e.tensor_tensor(
                    x[:, 2 * i2:2 * i2 + 2, :], bk[:, :].rearrange("p (i n) -> p i n", i=2),
                    x[:, 2 * i2:2 * i2 + 2, :], ALU.add), [p, xb[3]])
                ra.read_by(n, s)
                done.append(s)
            S["ont"] = p
            return done[-1]

        def moe(b, ready, S):
            A, X = b % 2, b % 3
            x = xa[:, X, :, :]
            nf = tmp[:, 0:1024].rearrange("p (i n) -> p i n", i=4)
            nrm = layernorm("f", x, stf, mvf, vef, rsf, nf, ready, [S["tmp"]])
            tp, tc_ = transposed("f", rf, nf, xf, [nrm[3]], [S["xf"]])
            gc = []
            for i in range(4):
                bk, busy, n = rf.take()

                def go(e, bk=bk, i=i):
                    for f in range(2):
                        r = e.matmul(bk[:, 0:400], xf[:, f, 128 * i:128 * i + 128], fg[:, f, :],
                                     start=(f == 0), stop=(f == 1))
                    return r
                p = pe("f", go, busy + tc_ + [L["fg"]], 1.36)
                c_ = act("f", lambda e, bk=bk, i=i: e.copy(xg[:, i, :], bk[:, 0:400]), [p, S["xg"]], 0.5)
                rf.read_by(n, c_)
                gc.append(c_)
            gl = xg[:, :, 320:400].rearrange("p i (g e) -> p i g e", e=5)
            cm = cmpt[:, :, :, :].rearrange("p (i g) a c -> p i g a c", i=4)
            prev = []
            for i in range(4):
                for e_ in range(5):
                    if e_ < 4:
                        prev.append(dve("f", lambda e, i=i, e_=e_: e.tensor_tensor(
                            cm[:, i, :, e_ + 1:5, e_], gl[:, i, :, e_:e_ + 1].to_broadcast([128, 16, 4 - e_]),
                            gl[:, i, :, e_ + 1:5], ALU.is_ge), [gc[3], c_cmp, S["cm"]], 0.13))
                    if e_ > 0:
                        prev.append(dve("f", lambda e, i=i, e_=e_: e.tensor_tensor(
                            cm[:, i, :, 0:e_, e_], gl[:, i, :, e_:e_ + 1].to_broadcast([128, 16, e_]),
                            gl[:, i, :, 0:e_], ALU.is_gt), [gc[3], c_cmp, S["cm"]], 0.13))
            rk = dve("f", lambda e: e.tensor_reduce(rank[:, :, :], cmpt[:, :, :, :], AX.X, ALU.add), [prev[-1]], 1.8)
            S["cm"] = rk
            mk = dve("f", lambda e: e.tensor_scalar(mask[:, :, :, :, :].rearrange("p i z h e -> p (i z h e)"),
                                                    rank[:, :, :].rearrange("p g e -> p (g e)"), 1.5, None,
                                                    ALU.is_lt), [rk, S["mask"]], 0.3)
            e1 = act("f", lambda e: e.activation(sg[:, :, :, :].rearrange("p i h e -> p i (h e)"),
                                                 xg[:, :, 320:360], ACT.Exp, scale=-1.0), [gc[3], S["sg"]], 0.35)
            s1 = dve("f", lambda e: e.tensor_scalar_add(sg2[:, :, :, :], sg[:, :, :, :], 1.0), [e1], 0.2)
            s2 = dve("f", lambda e: e.reciprocal(sg[:, :, :, :], sg2[:, :, :, :]), [s1], 0.3)
            s3 = dve("f", lambda e: e.tensor_tensor(wvx[:, :, :, :], sg[:, :, :, :], mask[:, :, 0, :, :], ALU.mult),
                     [s2, mk, S["wvx"]], 0.3)
            S["sg"] = s3
            tv = tmp[:, :].rearrange("p (i h d) -> p i h d", i=4, h=8)
            vm = None
            for e_ in range(5):
                first = e_ == 0
                for i in range(4):
                    to = v65[:, i, :, 0:64] if first else tv[:, i, :, :]
                    vm_ = pool("f", lambda e, to=to, e_=e_, i=i: e.tensor_tensor(
                        to, xg[:, i, 64 * e_:64 * e_ + 64].unsqueeze(1).to_broadcast([128, 8, 64]),
                        wvx[:, i, :, e_:e_ + 1].to_broadcast([128, 8, 64]), ALU.mult),
                        [s3, gc[3], tp[1], S["v65"] if first else vm], 1.1)
                if first:
                    vm = vm_
                else:
                    vm = pool("f", lambda e: e.tensor_tensor(v65[:, :, :, 0:64], v65[:, :, :, 0:64], tv, ALU.add),
                              [vm_], 4.3)
            S["xg"] = S["wvx"] = vm
            uacc = None
            last = None
            for hf in range(2):
                qd = []
                for z in range(2):
                    w, lw = ((fq, "fq"), (fk, "fk"))[z]
                    for cc in range(2):
                        bk, busy, n = rf.take()
                        col = 256 * hf + 128 * cc

                        def go(e, bk=bk, w=w, col=col):
                            for f in range(2):
                                r = e.matmul(bk[:, :], w[:, f, col:col + 128], xf[:, f, :], start=(f == 0), stop=(f == 1))
                            return r
                        p = pe("f", go, busy + tc_ + [L[lw]], 1.72)
                        last_proj = p
                        rd = []
                        for u in range(2):
                            s = 2 * cc + u
                            src = bk[64 * u:64 * u + 64, :]
                            free = [S["stk"][s]]
                            if z == 0:
                                a1 = act("f", lambda e, s=s, src=src: e.copy(q1[0:64, s, :], src), [p] + free)
                                a2 = act("f", lambda e, s=s, src=src: e.copy(q2[0:64, s, :], src), [p, c_q2z] + free)
                                d1 = dve("f", lambda e, s=s, src=src: e.tensor_tensor(
                                    q1[64:128, s, :], src, q1[0:64, s, :].bitcast(F32), ALU.subtract), [a1, a2] + free)
                            else:
                                a1 = act("f", lambda e, s=s, src=src: e.copy(k1[0:64, s, :], src), [p] + free)
                                a2 = act("f", lambda e, s=s, src=src: e.copy(k1[64:128, s, :], src), [p] + free)
                                d1 = dve("f", lambda e, s=s, src=src: e.tensor_tensor(
                                    k2[0:64, s, :], src, k1[0:64, s, :].bitcast(F32), ALU.subtract),
                                    [a1, a2, c_k2o] + free)
                            rd += [d1]
                            qd += [a2, d1]
                        rf.read_by(n, rd[-1], a2)
                mx = None
                for s in range(4):
                    for i in range(4):
                        bk, busy, n = rf.take()
                        p = pe("f", lambda e, bk=bk, s=s, i=i: e.matmul(
                            bk[:, :], q1[:, s, 128 * i:128 * i + 128], k1[:, s, :], start=True, stop=True), busy + qd)
                        mx = dve("f", lambda e, bk=bk, s=s, i=i: e.tensor_reduce(
                            mxf[:, i, s:s + 1], bk[:, :], AX.X, ALU.max, negate=True), [p, S["mxf"]])
                        rf.read_by(n, mx)
                bk, busy, n = rf.take()

                def go(e, bk=bk):
                    for i in range(4):
                        r = e.transpose(bk[0:4, 128 * i:128 * i + 128], mxf[:, i, :], ident[:, :])
                    return r
                p = pe("f", go, busy + [mx], 0.4)
                S["mxf"] = p
                h1 = act("f", lambda e, bk=bk: e.copy(mfh[:, 0, :], bk[0:4, :]), [p, S["mfh"]])
                l1 = dve("f", lambda e, bk=bk: e.tensor_tensor(mfh[:, 1, :], bk[0:4, :], mfh[:, 0, :].bitcast(F32),
                                                               ALU.subtract), [h1])
                rf.read_by(n, l1)
                w = dma("f", f"fw{hf}", maxf[A, hf].rearrange("s h n -> h s n"), mfh[:, :, :].bitcast(F32), [l1, S["maxf"][A, hf]])
                S["mfh"] = w
                row = dma("f", f"fr{hf}", q2[64:66, :, :].bitcast(F32), maxf[A, hf], [w, c_q2z] + S["stk"])
                S["maxf"][A, hf] = row
                for s in range(4):
                    h = 4 * hf + s
                    for kc in range(4):
                        bk, busy, n = rf.take()
                        ps = (4 * h + kc) % 3

                        def go(e, bk=bk, s=s, kc=kc):
                            e.matmul(bk[:, :], k1[:, s, 128 * kc:128 * kc + 128], q1[:, s, :], start=True, stop=False)
                            return e.matmul(bk[:, :], k2[:, s, 128 * kc:128 * kc + 128], q2[:, s, :],
                                            start=False, stop=True)
                        p = pe("f", go, busy + qd + [row, c_k2o], 0.44)
                        x_ = act("f", lambda e, bk=bk, ps=ps: e.activation(pf[:, ps, :], bk[:, :], ACT.Exp,
                                                                           scale=0.125), [p, S["pf"][ps]])
                        rf.read_by(n, x_)
                        pv = pe("fpv", lambda e, kc=kc, h=h, ps=ps: e.matmul(
                            of[0:65, :], v65[:, kc, h, :], pf[:, ps, :], start=(kc == 0), stop=(kc == 3)),
                            [x_, vm, c_v65] + ([S["of"]] if kc == 0 else []), 0.87)
                        S["pf"][ps] = pv
                    S["stk"][s] = p
                    S["v65"] = pv
                    ev = act("fpv", lambda e: e.copy(osb[:, :], of[0:65, :]), [pv, S["osb"]])
                    B = h % 2

                    def go(e):
                        for i in range(4):
                            r = e.transpose(of[:, 65 * i:65 * i + 65], osb[:, 128 * i:128 * i + 128], ident[0:65, 0:65])
                        return r
                    tr = pe("fpv", go, [ev], 0.4)
                    S["osb"] = tr
                    ov = of[:, 0:260].rearrange("p (i d) -> p i d", d=65)
                    rc = dve("fpv", lambda e, B=B, ov=ov: e.reciprocal(rcf[:, B, :], ov[:, :, 64]), [tr], 0.2)
                    ww = dve("fpv", lambda e, B=B, h=h: e.tensor_tensor(
                        w2[:, B, :, :], mask[:, :, 1, h, :], rcf[:, B, :].unsqueeze(2).to_broadcast([128, 4, 5]),
                        ALU.mult), [rc, mk], 0.15)
                    to = uu if h == 0 else pu
                    um = None
                    for i in range(4):
                        um = dve("fpv", lambda e, B=B, ov=ov, to=to, i=i: e.tensor_tensor(
                            to[:, i, :].rearrange("p (e k) -> p e k", k=64),
                            ov[:, i, 0:64].unsqueeze(1).to_broadcast([128, 5, 64]),
                            w2[:, B, i, :].unsqueeze(2).to_broadcast([128, 5, 64]), ALU.mult),
                            [ww, S["uu"] if h == 0 else S["pu"]], 0.45)
                    S["of"] = um
                    if h == 0:
                        uacc = um
                    else:
                        uacc = pool("fpv", lambda e: e.tensor_tensor(uu[:, :, :], uu[:, :, :], pu[:, :, :], ALU.add),
                                    [um, uacc], 2.7)
                        S["pu"] = uacc
                    S["mask"] = um
            S["xf"] = last_proj
            uc = []
            for k3, m in enumerate((128, 128, 64)):
                bk, busy, n = rf.take()

                def go(e, bk=bk, k3=k3, m=m):
                    for i in range(4):
                        r = e.transpose(bk[0:m, 128 * i:128 * i + 128], uu[:, i, 128 * k3:128 * k3 + m], ident[:, :])
                    return r
                p = pe("f", go, busy + [uacc], 0.5)
                c_ = act("f", lambda e, bk=bk, k3=k3, m=m: e.copy(ut[0:m, k3, :], bk[0:m, :]), [p, vm])
                rf.read_by(n, c_)
                uc.append(c_)
            S["uu"] = p
            for i2 in range(2):
                bk, busy, n = rf.take()

                def go(e, bk=bk, i2=i2):
                    for i in range(2):
                        tc = 2 * i2 + i
                        for k3, m in enumerate((128, 128, 64)):
                            r = e.matmul(bk[:, 256 * i:256 * i + 256], ut[0:m, k3, 128 * tc:128 * tc + 128],
                                         fo[0:m, k3, :], start=(k3 == 0), stop=(k3 == 2))
                    return r
                p = pe("f", go, busy + uc + [L["fo"], L["fo2"]], 2.6)
                s = dve("f", lambda e, bk=bk, i2=i2: e.tensor_tensor(
                    x[:, 2 * i2:2 * i2 + 2, :], bk[:, :].rearrange("p (i n) -> p i n", i=2),
                    x[:, 2 * i2:2 * i2 + 2, :], ALU.add), [p])
                rf.read_by(n, s)
            S["tmp"] = p
            return dma("st", f"out{X}", t["out"][b].rearrange("(c p) n -> p c n", p=128), x, [s])

        SA = {"xfree": [None] * 3, "xn_free": None, "xt_free": None, "pt": [None, None], "res": [None, None],
              "parts": {(a, z, c): None for a in range(2) for z in range(2) for c in range(2)},
              "stack": [None, None], "v32": None, "mxa": [None, None], "mp": None,
              "maxa": {(a, c): None for a in range(2) for c in range(2)}, "pa": [None, None], "oa": None,
              "t1": [None, None], "comb": None, "ont": None}
        SF = {"tmp": None, "xf": None, "xg": None, "cm": None, "mask": None, "sg": None, "wvx": None, "v65": None,
              "stk": [None] * 4, "mxf": None, "mfh": None, "maxf": {(a, c): None for a in range(2) for c in range(2)},
              "pf": [None] * 4, "of": None, "osb": None, "pu": None, "uu": None, "_": None}
        for b in range(t["nb"]):
            r = attn(b, SA)
            o = moe(b, r, SF)
            SA["xfree"][b % 3] = o

        Q.settle()
        eng_sem = {e: sem("e_" + e) for e in ENGINES}
        for e in ENGINES:
            n = 0
            for s in Q.order[e]:
                if s.dma is None and s.used:
                    n += 1
                    s.sem, s.value = eng_sem[e], n
        final = [(dma_sems[k], dma_counts[k][0]) for k in dma_counts]

        def emit(name):
            def body(e):
                seen = {}
                for s in Q.order[name]:
                    need = {}
                    for d in s.deps:
                        k = id(d.sem)
                        if seen.get(k, 0) < d.value and need.get(k, (None, 0))[1] < d.value:
                            need[k] = (d.sem, d.value)
                    for k, (m, v) in need.items():
                        e.wait_ge(m, v)
                        seen[k] = v
                    r = s.fn(e)
                    if s.dma is not None:
                        r.then_inc(s.sem, 16)
                    elif s.used:
                        r.then_inc(s.sem, 1)
                if name == "sync":
                    for m, v in final:
                        e.wait_ge(m, v)
            return body

        block = ctx.enter_context(nc.Block())
        block.sync(emit("sync"))
        block.tensor(emit("tensor"))
        block.scalar(emit("scalar"))
        block.vector(emit("vector"))
        block.gpsimd(emit("gpsimd"))


def kernel(L0_attn_x, L0_attn_Wk, L0_attn_Wq, L0_attn_Wv, L0_attn_Wo, L0_attn_bo, L0_ffn_Wq, L0_ffn_Wk, L0_ffn_Ws,
           L0_ffn_Wd, L0_ffn_Wv, L0_ffn_Wo):
    import concourse.bacc as bacc
    from concourse.bass_utils import run_bass_kernel_spmd

    def qk(w):
        return np.asarray(w).T.reshape(256, 2, 8, 16).transpose(0, 1, 3, 2).reshape(256, 256)

    arrays = {
        "x": np.asarray(L0_attn_x),
        "wq": qk(L0_attn_Wq),
        "wk": qk(L0_attn_Wk),
        "wv": np.asarray(L0_attn_Wv).T,
        "wo": np.asarray(L0_attn_Wo).T.reshape(2, 2, 4, 16, 256).transpose(0, 2, 1, 3, 4).reshape(256, 256),
        "bo": np.broadcast_to(np.asarray(L0_attn_bo), (128, 256)),
        "fq": np.asarray(L0_ffn_Wq),
        "fk": np.asarray(L0_ffn_Wk),
        "fg": np.concatenate([np.asarray(L0_ffn_Wv).transpose(1, 0, 2).reshape(256, 320), np.asarray(L0_ffn_Ws),
                              np.asarray(L0_ffn_Wd)], axis=1),
        "fo": np.asarray(L0_ffn_Wo).reshape(320, 256),
        "ident": np.eye(128, dtype=np.float32),
    }
    arrays = {k: np.ascontiguousarray(v) for k, v in arrays.items()}
    nb = arrays["x"].shape[0]
    nc = bacc.Bacc("TRN2", target_bir_lowering=False, num_devices=1)
    t = {k: nc.dram_tensor("in_" + k, v.shape, mybir.dt.from_np(v.dtype), kind="ExternalInput").ap()
         for k, v in arrays.items()}
    t["out"] = nc.dram_tensor("out_y", (nb, T, D), mybir.dt.float32, kind="ExternalOutput").ap()
    t["nb"] = nb
    program(nc, t)
    r = run_bass_kernel_spmd(nc, [{"in_" + k: v for k, v in arrays.items()}], core_ids=[0])
    return r.results[0]["out_y"]
```

```python
from contextlib import ExitStack

import numpy as np
import concourse.bass as bass
from concourse import mybir

NB, T, D = 32, 512, 256
ENGINES = ("sync", "tensor", "scalar", "vector", "gpsimd")
LAG = {"sync": 0.0, "tensor": 0.2, "scalar": 0.2, "vector": 0.17, "gpsimd": 0.15}


class Step:

    def __init__(self, eng, deps, fn, cost, dma):
        self.eng, self.deps, self.fn, self.cost, self.dma = eng, deps, fn, cost, dma
        self.used = False
        self.end = None
        self.sem = self.value = None


class Queues:

    def __init__(self):
        self.threads = {}
        self.order = {e: [] for e in ENGINES}

    def add(self, thread, eng, fn, deps, cost, dma=None):
        deps = [d for d in deps if d is not None]
        s = Step(eng, deps, fn, cost, dma)
        for d in deps:
            d.used = True
        self.threads.setdefault((eng, thread), []).append(s)
        return s

    def settle(self, rank):
        free = {e: 0.0 for e in ENGINES}
        head = {k: 0 for k in self.threads}
        live = {e: sorted((k for k in self.threads if k[0] == e), key=lambda k: rank[e][1].index(k[1])) for e in ENGINES}
        while True:
            best = None
            for e in ENGINES:
                can = []
                for k in live[e]:
                    q = self.threads[k]
                    if head[k] >= len(q):
                        continue
                    s = q[head[k]]
                    at = free[e]
                    for d in s.deps:
                        if d.end is None:
                            at = None
                            break
                        at = max(at, d.end)
                    if at is not None:
                        can.append((at, k, s))
                if can:
                    first = min(c[0] for c in can) + rank[e][0]
                    mine = next(c for c in can if c[0] <= first)
                    if best is None or mine[0] < best[0]:
                        best = mine
            if best is None:
                break
            at, k, s = best
            head[k] += 1
            hold, lag = (0.48, s.cost) if s.dma is not None else (s.cost, s.cost + LAG[k[0]])
            free[k[0]] = at + hold
            s.end = at + lag
            self.order[k[0]].append(s)
        assert all(head[k] == len(q) for k, q in self.threads.items()), "queues are stuck"


def program(nc, t):
    F32, BF, F32R = mybir.dt.float32, mybir.dt.bfloat16, mybir.dt.float32r
    ALU, ACT, AX = mybir.AluOpType, mybir.ActivationFunctionType, mybir.AxisListType
    ctx = ExitStack()
    Q = Queues()
    with ctx:
        def sb(name, shape, dt=F32):
            return ctx.enter_context(nc.sbuf_tensor("s_" + name, shape, dt))

        def sem(name):
            return ctx.enter_context(nc.semaphore("m_" + name))

        def dram(name, shape, dt):
            return nc.dram_tensor("w_" + name, shape, dt, kind="Internal").ap()

        ident = sb("ident", [128, 128])
        wq = sb("wq", [128, 2, 256])
        wk = sb("wk", [128, 2, 256])
        wv = sb("wv", [128, 2, 256])
        wo = sb("wo", [128, 2, 256])
        bo = sb("bo", [128, 256])
        fq = sb("fq", [128, 2, 512])
        fk = sb("fk", [128, 2, 512])
        fg = sb("fg", [128, 2, 400])
        fo = sb("fo", [128, 3, 256])
        nhalf = sb("nhalf", [128, 4])
        xa = sb("xa", [128, 3, 4, 256])
        xt = sb("xt", [128, 2, 512])
        sta = sb("sta", [128, 4, 6])
        mva = sb("mva", [128, 4, 2])
        vea = sb("vea", [128, 4])
        rsa = sb("rsa", [128, 4])
        pt = sb("pt", [128, 3, 512], BF)
        qs = sb("qs", [128, 2, 8, 512], BF)
        ks = sb("ks", [128, 2, 8, 512], BF)
        v32 = sb("v32", [128, 4, 16, 32])
        mxa = sb("mxa", [128, 2, 4, 8])
        mp = sb("mp", [8, 1, 3, 512], BF)
        pa = sb("pa", [128, 6, 512])
        t1 = sb("t1", [128, 2, 512])
        xn = sb("xn", [128, 4, 256])
        rca = sb("rca", [128, 2, 16])
        comb = sb("comb", [128, 512])[:, :]
        ont = sb("ont", [128, 2, 512])
        stf = sb("stf", [128, 4, 6])
        mvf = sb("mvf", [128, 4, 2])
        vef = sb("vef", [128, 4])
        rsf = sb("rsf", [128, 4])
        nf = sb("nf", [128, 4, 256])
        prod = sb("prod", [128, 4, 2, 64])
        xf = sb("xf", [128, 2, 512])
        xg = sb("xg", [128, 4, 400])
        cmpt = sb("cmpt", [128, 64, 5, 5], mybir.dt.uint8)
        rank = sb("rank", [128, 64, 5])
        mask = sb("mask", [128, 2, 4, 2, 8, 5])
        sg = sb("sg", [128, 4, 8, 5])
        sg2 = sb("sg2", [128, 4, 8, 5])
        wvx = sb("wvx", [128, 4, 8, 5])
        v65 = sb("v65", [128, 4, 8, 65])
        q1 = sb("q1", [128, 4, 512], F32R)
        q2 = sb("q2", [128, 4, 512], F32R)
        k1 = sb("k1", [128, 4, 512], F32R)
        k2 = sb("k2", [128, 4, 512], F32R)
        mxf = sb("mxf", [128, 2, 4, 2])
        mfh = sb("mfh", [2, 2, 512], F32R)
        pf = sb("pf", [128, 3, 512])
        osb = sb("osb", [65, 512])
        rcf = sb("rcf", [128, 2, 4])
        w2 = sb("w2", [128, 2, 4, 5])
        pu = sb("pu", [128, 2, 320])
        uu = sb("uu", [128, 4, 320])
        ut = sb("ut", [128, 3, 512])
        ots = sb("ots", [128, 4, 65])

        bank = [ctx.enter_context(nc.psum_tensor(f"bank{i}", [128, 512], F32)) for i in range(8)]

        parts = dram("parts", [2, 2, 2, 3, 128, 512], BF)
        maxa = dram("maxa", [2, 2, 3, 8, 512], BF)
        maxf = dram("maxf", [4, 2, 2, 512], F32)

        dma_sems, dma_counts = {}, {}

        def op(thread, eng, fn, deps=(), cost=0.3):
            return Q.add(thread, eng, fn, list(deps), cost)

        def pe(th, fn, deps=(), cost=0.22):
            return op(th, "tensor", fn, deps, cost)

        def act(th, fn, deps=(), cost=0.48):
            return op(th, "scalar", fn, deps, cost)

        def dve(th, fn, deps=(), cost=0.6):
            return op(th, "vector", fn, deps, cost)

        def pool(th, fn, deps=(), cost=1.0):
            return op(th, "gpsimd", fn, deps, cost)

        def dma(th, site, dst, src, deps=(), cost=2.5):
            if site not in dma_sems:
                dma_sems[site] = sem("d_" + site)
                dma_counts[site] = [0, None]
            last = dma_counts[site][1]
            s = Q.add(th, "sync", lambda e: e.dma_start(dst, src), list(deps) + [last], cost, dma=site)
            dma_counts[site][0] += 16
            dma_counts[site][1] = s
            s.sem, s.value = dma_sems[site], dma_counts[site][0]
            return s

        class Ring:

            def __init__(self, banks):
                self.banks, self.readers, self.n = banks, [[] for _ in banks], -1

            def take(self):
                self.n = (self.n + 1) % len(self.banks)
                return self.banks[self.n], self.readers[self.n], self.n

            def read_by(self, n, *steps):
                self.readers[n] = list(steps)

        rap, ram, rae = Ring(bank[0:1]), Ring(bank[1:2]), Ring(bank[2:3])
        rff, rfm, rfe = Ring(bank[3:4]), Ring(bank[4:5]), Ring(bank[5:6])
        oa, of = bank[6], bank[7]

        loads = []
        for name, dst, src in [
            ("ident", ident[:, :], t["ident"]),
            ("wq", wq[:, :, :], t["wq"].rearrange("(c p) n -> p c n", p=128)),
            ("wk", wk[:, :, :], t["wk"].rearrange("(c p) n -> p c n", p=128)),
            ("wv", wv[:, :, :], t["wv"].rearrange("(c p) n -> p c n", p=128)),
            ("wo", wo[:, :, :], t["wo"].rearrange("(c p) n -> p c n", p=128)),
            ("bo", bo[:, :], t["bo"]),
            ("fq", fq[:, :, :], t["fq"].rearrange("(c p) n -> p c n", p=128)),
            ("fk", fk[:, :, :], t["fk"].rearrange("(c p) n -> p c n", p=128)),
            ("fg", fg[:, :, :], t["fg"].rearrange("(c p) n -> p c n", p=128)),
            ("fo", fo[:, 0:2, :], t["fo"][0:256, :].rearrange("(c p) n -> p c n", p=128)),
            ("fo2", fo[0:64, 2, :], t["fo"][256:320, :]),
        ]:
            loads.append(dma("ld", name, dst, src))
        L = dict(zip(["ident", "wq", "wk", "wv", "wo", "bo", "fq", "fk", "fg", "fo", "fo2"], loads))
        c_half = pool("c", lambda e: e.memset(nhalf[:, :], -0.5))
        c_v32 = pool("c", lambda e: e.memset(v32[:, :, :, 16:32], 1.0))
        c_ks = dve("c", lambda e: e.memset(ks[96:99, :, :, :], 1.0), cost=8)
        c_v65 = pool("c", lambda e: e.memset(v65[:, :, :, 64:65], 1.0))
        c_k2z = dve("c", lambda e: e.memset(k2[64:128, :, :].bitcast(F32), 0.0))
        c_k2o = dve("c", lambda e: e.memset(k2[64:66, :, :].bitcast(F32), 1.0), [c_k2z])
        c_q2z = dve("c", lambda e: e.memset(q2[64:128, :, :].bitcast(F32), 0.0))
        c_cmp = dve("c", lambda e: e.memset(cmpt[:, :, :, :], 0.0))

        def layernorm(th, x, st, mv, ve, rs, out, ready, free):
            a = [dve(th, lambda e, i=i: e.bn_stats(st[:, i, :], x[:, i, :]), [ready], 0.35) for i in range(4)]
            g = [dve(th, lambda e, i=i: e.bn_aggr(mv[:, i, :], st[:, i, :]), [a[i]], 0.12) for i in range(4)]
            v = dve(th, lambda e: e.tensor_scalar_add(ve[:, :], mv[:, :, 1], 1e-5), [g[3]], 0.1)
            r = pool(th, lambda e: e.tensor_tensor(rs[:, :], ve[:, :], nhalf[:, :], ALU.pow), [v, c_half], 1.0)
            return [dve(th, lambda e, i=i: e.tensor_scalar(out[:, i, :], x[:, i, :], mv[:, i, 0:1], rs[:, i:i + 1],
                                                          ALU.subtract, ALU.mult), [r] + free, 0.32)
                    for i in range(4)]

        def transposed(th, ring, src, dst, ready, free):
            out = []
            for f in range(2):
                b, busy, n = ring.take()

                def go(e, b=b, f=f):
                    for i in range(4):
                        r = e.transpose(b[:, 128 * i:128 * i + 128], src[:, i, 128 * f:128 * f + 128], ident[:, :])
                    return r
                p = pe(th, go, busy + ready + [L["ident"]], 0.5)
                c = act(th, lambda e, b=b, f=f: e.copy(dst[:, f, :], b[:, :]), [p] + free)
                ring.read_by(n, c)
                out.append((p, c))
            return [p for p, _ in out], [c for _, c in out]

        def attn(b, S):
            A, X = b % 2, b % 3
            x = xa[:, X, :, :]
            ld = dma("ld", f"x{X}", x, t["x"][b].rearrange("(c p) n -> p c n", p=128), [S["xfree"][X]])
            nrm = layernorm("ap", x, sta, mva, vea, rsa, xn, ld, [S["xn"]])
            xb = [pool("ap", lambda e, i=i: e.tensor_tensor(x[:, i, :], x[:, i, :], bo[:, :], ALU.add),
                       [nrm[3], L["bo"]], 0.7) for i in range(4)]
            tp, tc_ = transposed("ap", rap, xn, xt, nrm, S["xt"])
            S["xn"] = tp[1]
            stacked, rows, proj = {}, [], []
            for c in range(2):
                for z, (w, lw, dst) in enumerate(((wq, "wq", qs), (wk, "wk", ks))):
                    bk, busy, n = rap.take()

                    def go(e, bk=bk, w=w, c=c):
                        for f in range(2):
                            r = e.matmul(bk[:, :], w[:, f, 128 * c:128 * c + 128], xt[:, f, :],
                                         start=(f == 0), stop=(f == 1))
                        return r
                    p = pe("ap", go, busy + tc_ + [L[lw]], 1.72)
                    proj.append(p)
                    hi = act("ap", lambda e, bk=bk: e.copy(pt[:, 0, :], bk[:, :]), [p, S["pt"]])
                    r1 = dve("ap", lambda e, bk=bk: e.tensor_tensor(bk[:, :], bk[:, :], pt[:, 0, :], ALU.subtract), [hi])
                    mid = act("ap", lambda e, bk=bk: e.copy(pt[:, 1, :], bk[:, :]), [r1])
                    lo = dve("ap", lambda e, bk=bk: e.tensor_tensor(pt[:, 2, :], bk[:, :], pt[:, 1, :], ALU.subtract),
                             [mid])
                    rap.read_by(n, lo)
                    st = dma("ap", f"pw{z}{c}", parts[A, z, c].rearrange("s p n -> p s n"), pt[:, :, :],
                             [lo] + S["parts"][A, z, c])
                    S["pt"] = st
                    sd = parts[A, z, c].rearrange("s (d h) n -> (s d) h n", h=8)
                    cuts = [(0, 0, 48), (48, 0, 32), (80, 0, 16)] if z == 0 else \
                        [(0, 0, 16), (16, 0, 16), (32, 0, 16), (48, 16, 16), (64, 16, 16), (80, 32, 16)]
                    got = [dma("ap", f"pr{z}{c}{j}", dst[to:to + k, c, :, :], sd[fr:fr + k, :, :], [st] + S["stack"][c])
                           for j, (to, fr, k) in enumerate(cuts)]
                    stacked[z, c] = got
                    S["parts"][A, z, c] = got
                for h in range(8):
                    for i in range(4):
                        bk, busy, n = ram.take()
                        p = pe("am", lambda e, bk=bk, c=c, h=h, i=i: e.matmul(
                            bk[:, :], qs[0:96, c, h, 128 * i:128 * i + 128], ks[0:96, c, h, :], start=True, stop=True),
                            busy + stacked[0, c] + stacked[1, c])
                        mx = dve("am", lambda e, bk=bk, c=c, h=h, i=i: e.tensor_reduce(
                            mxa[:, c, i, h:h + 1], bk[:, :], AX.X, ALU.max, negate=True), [p, S["mxa"][c]])
                        ram.read_by(n, mx)
                bk, busy, n = ram.take()

                def go(e, bk=bk, c=c):
                    for i in range(4):
                        r = e.transpose(bk[0:8, 128 * i:128 * i + 128], mxa[:, c, i, :], ident[:, :])
                    return r
                p = pe("am", go, busy + [mx], 0.45)
                S["mxa"][c] = p
                h1 = act("am", lambda e, bk=bk: e.copy(mp[:, 0, 0, :], bk[0:8, :]), [p, S["mp"]])
                r1 = dve("am", lambda e, bk=bk: e.tensor_tensor(bk[0:8, :], bk[0:8, :], mp[:, 0, 0, :], ALU.subtract), [h1])
                m1 = act("am", lambda e, bk=bk: e.copy(mp[:, 0, 1, :], bk[0:8, :]), [r1])
                l1 = dve("am", lambda e, bk=bk: e.tensor_tensor(mp[:, 0, 2, :], bk[0:8, :], mp[:, 0, 1, :], ALU.subtract),
                         [m1])
                ram.read_by(n, l1)
                w = dma("am", f"mw{c}", maxa[A, c].rearrange("s h n -> h s n"), mp[:, 0, :, :], [l1, S["maxa"][A, c]])
                S["mp"] = w
                g = dma("am", f"mr{c}", qs[96:99, c, :, :], maxa[A, c], [w] + S["stack"][c])
                S["maxa"][A, c] = g
                rows.append(g)
            vd = []
            for i2 in range(2):
                bk, busy, n = rae.take()

                def go(e, bk=bk, i2=i2):
                    for i in range(2):
                        for f in range(2):
                            tc = 2 * i2 + i
                            r = e.matmul(bk[:, 256 * i:256 * i + 256], xt[:, f, 128 * tc:128 * tc + 128], wv[:, f, :],
                                         start=(f == 0), stop=(f == 1))
                    return r
                p = pe("av", go, busy + tc_ + [L["wv"]], 1.74)
                c_ = act("av", lambda e, bk=bk, i2=i2: e.copy(
                    v32[:, 2 * i2:2 * i2 + 2, :, 0:16], bk[:, :].rearrange("p (i h d) -> p i h d", i=2, h=16)),
                    [p, c_v32, S["v32"]])
                rae.read_by(n, c_)
                vd.append(c_)
            S["xt"] = [p, proj[-1]]
            outs = []
            for j in range(4):
                c = j // 2
                for kc in range(4):
                    ex, slots = [], []
                    for g in range(4):
                        h = 4 * (j % 2) + g
                        S["pn"] = (S["pn"] + 1) % 6
                        slot = S["pn"]
                        slots.append(slot)
                        bk, busy, n = rae.take()
                        p = pe("ae", lambda e, bk=bk, c=c, h=h, kc=kc: e.matmul(
                            bk[:, :], ks[0:99, c, h, 128 * kc:128 * kc + 128], qs[0:99, c, h, :],
                            start=True, stop=True), busy + [rows[c], c_ks])
                        x_ = act("ae", lambda e, bk=bk, slot=slot: e.activation(
                            pa[:, slot, :], bk[:, :], ACT.Exp, scale=0.0625), [p, S["pa"][slot]], 0.48)
                        rae.read_by(n, x_)
                        ex.append(x_)

                    def go(e, slots=tuple(slots), kc=kc, j=j):
                        for g in range(4):
                            r = e.matmul(oa[32 * g:32 * g + 32, :], v32[:, kc, 4 * j + g, :], pa[:, slots[g], :],
                                         start=(kc == 0), stop=(kc == 3))
                        return r
                    pv = pe("apv", go, ex + vd + ([S["oa"]] if kc == 0 else []), 0.98)
                    for slot in slots:
                        S["pa"][slot] = pv
                S["stack"][c] = [p]
                B, a = j % 2, j % 2
                tr = dve("apv", lambda e, B=B: e.transpose(t1[:, B, :], oa[:, :]), [pv, S["t1"][B]])
                S["oa"] = tr
                t4 = t1[:, B, :].rearrange("p (k j) -> p k j", j=32)
                rc = dve("apv", lambda e, B=B, t4=t4: e.reciprocal(rca[:, B, :], t4[:, :, 16]), [tr], 0.15)
                ml = dve("apv", lambda e, B=B, t4=t4, a=a: e.tensor_tensor(
                    comb.rearrange("p (k j) -> p k j", j=32)[:, :, 16 * a:16 * a + 16], t4[:, :, 0:16],
                    rca[:, B, :].unsqueeze(2).to_broadcast([128, 16, 16]), ALU.mult), [rc, S["comb"]], 0.35)
                S["t1"][B] = ml
                if a:
                    tt = dve("apv", lambda e, j=j: e.transpose(ont[:, j // 2, :], comb), [ml, S["ont"]])
                    S["comb"] = tt
                    outs.append(tt)
            S["v32"] = pv
            for i2 in range(2):
                bk, busy, n = rae.take()

                def go(e, bk=bk, i2=i2):
                    for i in range(2):
                        for f in range(2):
                            tc = 2 * i2 + i
                            r = e.matmul(bk[:, 256 * i:256 * i + 256], ont[:, f, 128 * tc:128 * tc + 128], wo[:, f, :],
                                         start=(f == 0), stop=(f == 1))
                    return r
                p = pe("ae", go, busy + outs + [L["wo"]], 1.74)
                s = dve("ae", lambda e, bk=bk, i2=i2: e.tensor_tensor(
                    x[:, 2 * i2:2 * i2 + 2, :], bk[:, :].rearrange("p (i n) -> p i n", i=2),
                    x[:, 2 * i2:2 * i2 + 2, :], ALU.add), [p, xb[3]])
                rae.read_by(n, s)
            S["ont"] = p
            return s

        def moe(b, ready, S):
            M, X = b % 2, b % 3
            x = xa[:, X, :, :]
            nrm = layernorm("fq", x, stf, mvf, vef, rsf, nf, ready, [S["nf"]])
            tp, tc_ = transposed("fq", rff, nf, xf, nrm, S["xf"])
            S["nf"] = tp[1]
            gc = []
            for i in range(4):
                bk, busy, n = rff.take()

                def go(e, bk=bk, i=i):
                    for f in range(2):
                        r = e.matmul(bk[:, 0:400], xf[:, f, 128 * i:128 * i + 128], fg[:, f, :],
                                     start=(f == 0), stop=(f == 1))
                    return r
                p = pe("fq", go, busy + tc_ + [L["fg"]], 1.36)
                c_ = act("fq", lambda e, bk=bk, i=i: e.copy(xg[:, i, :], bk[:, 0:400]), [p, S["xg"], S["cm"]], 0.4)
                rff.read_by(n, c_)
                gc.append(c_)
            gl = xg[:, :, 320:400].rearrange("p i (g e) -> p i g e", e=5)
            cm = cmpt[:, :, :, :].rearrange("p (i g) a c -> p i g a c", i=4)
            prev = []
            for e_ in range(5):
                if e_ < 4:
                    prev.append(dve("fq", lambda e, e_=e_: e.tensor_tensor(
                        cm[:, :, :, e_ + 1:5, e_], gl[:, :, :, e_:e_ + 1].to_broadcast([128, 4, 16, 4 - e_]),
                        gl[:, :, :, e_ + 1:5], ALU.is_ge), gc + [c_cmp, S["cm"]], 0.07 * (5 - e_)))
                if e_ > 0:
                    prev.append(dve("fq", lambda e, e_=e_: e.tensor_tensor(
                        cm[:, :, :, 0:e_, e_], gl[:, :, :, e_:e_ + 1].to_broadcast([128, 4, 16, e_]),
                        gl[:, :, :, 0:e_], ALU.is_gt), gc + [c_cmp, S["cm"]], 0.07 * (e_ + 1)))
            rk = dve("fq", lambda e: e.tensor_reduce(rank[:, :, :], cmpt[:, :, :, :], AX.X, ALU.add), [prev[-1]], 1.74)
            S["cm"] = rk
            mk = dve("fq", lambda e: e.tensor_scalar(mask[:, M, :, :, :, :].rearrange("p i z h e -> p (i z h e)"),
                                                     rank[:, :, :].rearrange("p g e -> p (g e)"), 1.5, None,
                                                     ALU.is_lt), [rk, S["mask"][M]], 0.3)
            e1 = act("fq", lambda e: e.activation(sg[:, :, :, :].rearrange("p i h e -> p i (h e)"),
                                                  xg[:, :, 320:360], ACT.Exp, scale=-1.0), [gc[3], S["sg"]], 0.23)
            s1 = dve("fq", lambda e: e.tensor_scalar_add(sg2[:, :, :, :], sg[:, :, :, :], 1.0), [e1], 0.2)
            s2 = dve("fq", lambda e: e.reciprocal(sg[:, :, :, :], sg2[:, :, :, :]), [s1], 1.07)
            s3 = dve("fq", lambda e: e.tensor_tensor(wvx[:, :, :, :], sg[:, :, :, :], mask[:, M, :, 0, :, :], ALU.mult),
                     [s2, mk, S["wvx"]], 0.25)
            S["sg"] = s3
            qk = {}

            def front(pair):
                qd = []
                for z in range(2):
                    w, lw = ((fq, "fq"), (fk, "fk"))[z]
                    bk, busy, n = rff.take()
                    col = 128 * pair

                    def go(e, bk=bk, w=w, col=col):
                        for f in range(2):
                            r = e.matmul(bk[:, :], w[:, f, col:col + 128], xf[:, f, :], start=(f == 0), stop=(f == 1))
                        return r
                    p = pe("fq", go, busy + tc_ + [L[lw]], 1.72)
                    S["proj"] = p
                    a_ = []
                    for u in range(2):
                        s = 2 * (pair % 2) + u
                        src = bk[64 * u:64 * u + 64, :]
                        free = S["stk"][s]
                        up, dn = ((q1[0:64, s, :], q2[0:64, s, :]), (k1[0:64, s, :], k1[64:128, s, :]))[z]
                        a1 = act("fq", lambda e, up=up, src=src: e.copy(up, src), [p] + free, 0.48)
                        a2 = act("fq", lambda e, dn=dn, src=src: e.copy(dn, src), [p, c_q2z] + free, 0.48)
                        a_ += [a1, a2]
                    for u in range(2):
                        s = 2 * (pair % 2) + u
                        src = bk[64 * u:64 * u + 64, :]
                        up, to = ((q1[0:64, s, :], q1[64:128, s, :]), (k1[0:64, s, :], k2[0:64, s, :]))[z]
                        d1 = dve("fq", lambda e, up=up, src=src, to=to: e.tensor_tensor(
                            to, src, up.bitcast(F32), ALU.subtract), a_ + S["stk"][s])
                        qd += [d1]
                    rff.read_by(n, d1)
                    qd += a_
                B = pair % 2
                for u in range(2):
                    s = 2 * B + u
                    for i in range(4):
                        bk, busy, n = rfm.take()
                        p = pe("fm", lambda e, bk=bk, s=s, i=i: e.matmul(
                            bk[:, :], q1[:, s, 128 * i:128 * i + 128], k1[:, s, :], start=True, stop=True), busy + qd)
                        mx = dve("fm", lambda e, bk=bk, B=B, u=u, i=i: e.tensor_reduce(
                            mxf[:, B, i, u:u + 1], bk[:, :], AX.X, ALU.max, negate=True), [p, S["mxf"][B]])
                        rfm.read_by(n, mx)
                bk, busy, n = rfm.take()

                def go(e, bk=bk):
                    for i in range(4):
                        r = e.transpose(bk[0:2, 128 * i:128 * i + 128], mxf[:, B, i, :], ident[:, :])
                    return r
                p = pe("fm", go, busy + [mx], 0.43)
                S["mxf"][B] = p
                h1 = act("fm", lambda e, bk=bk: e.copy(mfh[:, 0, :], bk[0:2, :]), [p, S["mfh"]])
                l1 = dve("fm", lambda e, bk=bk: e.tensor_tensor(mfh[:, 1, :], bk[0:2, :], mfh[:, 0, :].bitcast(F32),
                                                                ALU.subtract), [h1])
                rfm.read_by(n, l1)
                w = dma("fm", f"fw{pair}", maxf[pair].rearrange("s h n -> h s n"), mfh[:, :, :].bitcast(F32),
                        [l1, S["maxf"][pair]])
                S["mfh"] = w
                row = dma("fm", f"fr{pair}", q2[64:66, 2 * B:2 * B + 2, :].bitcast(F32), maxf[pair],
                          [w, c_q2z] + S["stk"][2 * B] + S["stk"][2 * B + 1])
                S["maxf"][pair] = row
                qk[pair] = qd + [row]

            def values(pair):
                last = None
                for e_ in range(5):
                    to = v65[:, :, 2 * pair:2 * pair + 2, 0:64] if e_ == 0 else prod[:, :, :, :]
                    xv = xg[:, :, 64 * e_:64 * e_ + 64]
                    m = pool("fv", lambda e, to=to, xv=xv, e_=e_: e.tensor_tensor(
                        to, xv.unsqueeze(2).to_broadcast([128, 4, 2, 64]),
                        wvx[:, :, 2 * pair:2 * pair + 2, e_:e_ + 1].to_broadcast([128, 4, 2, 64]), ALU.mult),
                        [s3] + gc + [S["v65"][pair] if e_ == 0 else last], 1.0)
                    if e_ == 0:
                        last = m
                    else:
                        vv = v65[:, :, 2 * pair:2 * pair + 2, 0:64]
                        last = pool("fv", lambda e, vv=vv: e.tensor_tensor(vv, vv, prod[:, :, :, :], ALU.add), [m], 1.22)
                return last

            def heads(pair, vm):
                for u in range(2):
                    h, s = 2 * pair + u, 2 * (pair % 2) + u
                    for kc in range(4):
                        bk, busy, n = rfe.take()
                        ps = (4 * h + kc) % 3

                        def go(e, bk=bk, s=s, kc=kc):
                            e.matmul(bk[:, :], k1[:, s, 128 * kc:128 * kc + 128], q1[:, s, :], start=True, stop=False)
                            return e.matmul(bk[:, :], k2[:, s, 128 * kc:128 * kc + 128], q2[:, s, :],
                                            start=False, stop=True)
                        p = pe("fe", go, busy + qk[pair] + [c_k2o], 0.44)
                        x_ = act("fe", lambda e, bk=bk, ps=ps: e.activation(pf[:, ps, :], bk[:, :], ACT.Exp,
                                                                            scale=0.125), [p, S["pf"][ps]], 0.48)
                        rfe.read_by(n, x_)
                        pv = pe("fpv", lambda e, kc=kc, h=h, ps=ps: e.matmul(
                            of[0:65, :], v65[:, kc, h, :], pf[:, ps, :], start=(kc == 0), stop=(kc == 3)),
                            [x_, vm, c_v65] + ([S["of"]] if kc == 0 else []), 0.87)
                        S["pf"][ps] = pv
                    S["stk"][s] = [p]
                    ev = act("fpv", lambda e: e.copy(osb[:, :], of[0:65, :]), [pv, S["osb"]], 0.48)
                    B = h % 2

                    def go(e):
                        for i in range(4):
                            r = e.transpose(of[:, 65 * i:65 * i + 65], osb[:, 128 * i:128 * i + 128], ident[0:65, 0:65])
                        return r
                    tr = pe("fpv", go, [ev], 0.24)
                    S["osb"] = tr
                    ov = of[:, 0:260].rearrange("p (i d) -> p i d", d=65)
                    oc = act("fpv", lambda e, ov=ov: e.copy(ots[:, :, :], ov), [tr, S["ots"]], 0.27)
                    S["of"] = oc
                    rc = dve("fpv", lambda e, B=B: e.reciprocal(rcf[:, B, :], ots[:, :, 64]), [oc], 0.1)
                    ww = dve("fpv", lambda e, B=B, h=h: e.tensor_tensor(
                        w2[:, B, :, :], mask[:, M, :, 1, h, :], rcf[:, B, :].unsqueeze(2).to_broadcast([128, 4, 5]),
                        ALU.mult), [rc, mk], 0.12)
                    for i2 in range(2):
                        first = h == 0
                        cut = slice(2 * i2, 2 * i2 + 2)
                        to = uu[:, cut, :] if first else pu[:, :, :]
                        um = pool("fpv", lambda e, B=B, to=to, cut=cut: e.tensor_tensor(
                            to.rearrange("p i (e k) -> p i e k", k=64),
                            ots[:, cut, 0:64].unsqueeze(2).to_broadcast([128, 2, 5, 64]),
                            w2[:, B, cut, :].unsqueeze(3).to_broadcast([128, 2, 5, 64]), ALU.mult),
                            [ww, S["uu"] if first else S["ua"][1]], 1.22)
                        if first:
                            S["ua"][i2] = um
                        else:
                            S["ua"][i2] = pool("fpv", lambda e, cut=cut: e.tensor_tensor(
                                uu[:, cut, :], uu[:, cut, :], pu[:, :, :], ALU.add), [um, S["ua"][i2]], 1.5)
                            S["ua"][1] = S["ua"][i2]
                    S["ots"] = um
                    S["mask"][M] = ww
                S["v65"][pair] = pv

            vals = []
            for pair in range(4):
                front(pair)
                vals.append(values(pair))
                heads(pair, vals[pair])
            S["xg"] = S["wvx"] = vals[3]
            S["xf"] = [S["proj"]]
            uc = []
            for k3, m in enumerate((128, 128, 64)):
                bk, busy, n = rfe.take()

                def go(e, bk=bk, k3=k3, m=m):
                    for i in range(4):
                        r = e.transpose(bk[0:m, 128 * i:128 * i + 128], uu[:, i, 128 * k3:128 * k3 + m], ident[:, :])
                    return r
                p = pe("fe", go, busy + S["ua"], 0.48)
                c_ = act("fe", lambda e, bk=bk, k3=k3, m=m: e.copy(ut[0:m, k3, :], bk[0:m, :]), [p, S["ut"]], 0.48)
                rfe.read_by(n, c_)
                uc.append(c_)
            S["uu"] = p
            for i2 in range(2):
                bk, busy, n = rfe.take()

                def go(e, bk=bk, i2=i2):
                    for i in range(2):
                        tc = 2 * i2 + i
                        for k3, m in enumerate((128, 128, 64)):
                            r = e.matmul(bk[:, 256 * i:256 * i + 256], ut[0:m, k3, 128 * tc:128 * tc + 128],
                                         fo[0:m, k3, :], start=(k3 == 0), stop=(k3 == 2))
                    return r
                p = pe("fe", go, busy + uc + [L["fo"], L["fo2"]], 2.6)
                s = dve("fe", lambda e, bk=bk, i2=i2: e.tensor_tensor(
                    x[:, 2 * i2:2 * i2 + 2, :], bk[:, :].rearrange("p (i n) -> p i n", i=2),
                    x[:, 2 * i2:2 * i2 + 2, :], ALU.add), [p])
                rfe.read_by(n, s)
            S["ut"] = p
            return dma("st", f"out{X}", t["out"][b].rearrange("(c p) n -> p c n", p=128), x, [s])

        SA = {"xfree": [None] * 3, "xn": None, "xt": [], "pt": None, "stack": [[], []], "v32": None,
              "parts": {(a, z, c): [] for a in range(2) for z in range(2) for c in range(2)},
              "mxa": [None, None], "mp": None, "maxa": {(a, c): None for a in range(2) for c in range(2)},
              "pa": [None] * 6, "pn": 0, "oa": None, "t1": [None, None], "comb": None, "ont": None}
        SF = {"nf": None, "xf": [], "xg": None, "cm": None, "mask": [None] * 2, "sg": None, "wvx": None,
              "v65": [None] * 4, "stk": [[] for _ in range(4)], "mxf": [None] * 2, "mfh": None, "maxf": [None] * 4,
              "pf": [None] * 3, "of": None, "osb": None, "ots": None, "pu": [None] * 2, "ua": [None] * 4, "uu": None, "ut": None}
        for b in range(t["nb"]):
            r = attn(b, SA)
            o = moe(b, r, SF)
            SA["xfree"][b % 3] = o

        Q.settle({
            "sync": (0.00, "am ap fm ld st".split()),
            "tensor": (0.10, "am ae fm fq apv fe ap av fpv".split()),
            "scalar": (0.00, "fpv ae fe ap fq fm am av".split()),
            "vector": (0.00, "am ae ap fpv fm fq c fe apv".split()),
            "gpsimd": (0.55, "fpv ap c fq fv".split()),
        })
        eng_sem = {e: sem("e_" + e) for e in ENGINES}
        for e in ENGINES:
            n = 0
            for s in Q.order[e]:
                if s.dma is None and s.used:
                    n += 1
                    s.sem, s.value = eng_sem[e], n
        final = [(dma_sems[k], dma_counts[k][0]) for k in dma_counts]

        def emit(name):
            def body(e):
                seen = {}
                for s in Q.order[name]:
                    need = {}
                    for d in s.deps:
                        k = id(d.sem)
                        if seen.get(k, 0) < d.value and need.get(k, (None, 0))[1] < d.value:
                            need[k] = (d.sem, d.value)
                    for k, (m, v) in need.items():
                        e.wait_ge(m, v)
                        seen[k] = v
                    r = s.fn(e)
                    if s.dma is not None:
                        r.then_inc(s.sem, 16)
                    elif s.used:
                        r.then_inc(s.sem, 1)
                if name == "sync":
                    for m, v in final:
                        e.wait_ge(m, v)
            return body

        block = ctx.enter_context(nc.Block())
        block.sync(emit("sync"))
        block.tensor(emit("tensor"))
        block.scalar(emit("scalar"))
        block.vector(emit("vector"))
        block.gpsimd(emit("gpsimd"))


def kernel(L0_attn_x, L0_attn_Wk, L0_attn_Wq, L0_attn_Wv, L0_attn_Wo, L0_attn_bo, L0_ffn_Wq, L0_ffn_Wk, L0_ffn_Ws,
           L0_ffn_Wd, L0_ffn_Wv, L0_ffn_Wo):
    import concourse.bacc as bacc
    from concourse.bass_utils import run_bass_kernel_spmd

    def qk(w):
        return np.asarray(w).T.reshape(256, 2, 8, 16).transpose(0, 1, 3, 2).reshape(256, 256)

    arrays = {
        "x": np.asarray(L0_attn_x),
        "wq": qk(L0_attn_Wq),
        "wk": qk(L0_attn_Wk),
        "wv": np.asarray(L0_attn_Wv).T,
        "wo": np.asarray(L0_attn_Wo).T.reshape(2, 2, 4, 16, 256).transpose(0, 2, 1, 3, 4).reshape(256, 256),
        "bo": np.broadcast_to(np.asarray(L0_attn_bo), (128, 256)),
        "fq": np.asarray(L0_ffn_Wq),
        "fk": np.asarray(L0_ffn_Wk),
        "fg": np.concatenate([np.asarray(L0_ffn_Wv).transpose(1, 0, 2).reshape(256, 320), np.asarray(L0_ffn_Ws),
                              np.asarray(L0_ffn_Wd)], axis=1),
        "fo": np.asarray(L0_ffn_Wo).reshape(320, 256),
        "ident": np.eye(128, dtype=np.float32),
    }
    arrays = {k: np.ascontiguousarray(v) for k, v in arrays.items()}
    nb = arrays["x"].shape[0]
    nc = bacc.Bacc("TRN2", target_bir_lowering=False, num_devices=1)
    t = {k: nc.dram_tensor("in_" + k, v.shape, mybir.dt.from_np(v.dtype), kind="ExternalInput").ap()
         for k, v in arrays.items()}
    t["out"] = nc.dram_tensor("out_y", (nb, T, D), mybir.dt.float32, kind="ExternalOutput").ap()
    t["nb"] = nb
    program(nc, t)
    r = run_bass_kernel_spmd(nc, [{"in_" + k: v for k, v in arrays.items()}], core_ids=[0])
    return r.results[0]["out_y"]
```

```python
from contextlib import ExitStack

import numpy as np
import concourse.bass as bass
from concourse import mybir

NB, T, D = 32, 512, 256
ENGINES = ("sync", "tensor", "scalar", "vector", "gpsimd")
LAG = {"sync": 0.0, "tensor": 0.2, "scalar": 0.2, "vector": 0.17, "gpsimd": 0.15}


class Step:

    def __init__(self, eng, deps, fn, cost, dma):
        self.eng, self.deps, self.fn, self.cost, self.dma = eng, deps, fn, cost, dma
        self.used = False
        self.end = None
        self.sem = self.value = None


class Queues:

    def __init__(self):
        self.threads = {}
        self.order = {e: [] for e in ENGINES}

    def add(self, thread, eng, fn, deps, cost, dma=None):
        deps = [d for d in deps if d is not None]
        s = Step(eng, deps, fn, cost, dma)
        for d in deps:
            d.used = True
        self.threads.setdefault((eng, thread), []).append(s)
        return s

    def settle(self, rank):
        free = {e: 0.0 for e in ENGINES}
        head = {k: 0 for k in self.threads}
        live = {e: sorted((k for k in self.threads if k[0] == e), key=lambda k: rank[e][1].index(k[1])) for e in ENGINES}
        while True:
            best = None
            for e in ENGINES:
                can = []
                for k in live[e]:
                    q = self.threads[k]
                    if head[k] >= len(q):
                        continue
                    s = q[head[k]]
                    at = free[e]
                    for d in s.deps:
                        if d.end is None:
                            at = None
                            break
                        at = max(at, d.end)
                    if at is not None:
                        can.append((at, k, s))
                if can:
                    first = min(c[0] for c in can) + rank[e][0]
                    mine = next(c for c in can if c[0] <= first)
                    if best is None or mine[0] < best[0]:
                        best = mine
            if best is None:
                break
            at, k, s = best
            head[k] += 1
            hold, lag = (0.48, s.cost) if s.dma is not None else (s.cost, s.cost + LAG[k[0]])
            free[k[0]] = at + hold
            s.end = at + lag
            self.order[k[0]].append(s)
        assert all(head[k] == len(q) for k, q in self.threads.items()), "queues are stuck"


def program(nc, t):
    F32, BF, F32R = mybir.dt.float32, mybir.dt.bfloat16, mybir.dt.float32r
    ALU, ACT, AX = mybir.AluOpType, mybir.ActivationFunctionType, mybir.AxisListType
    ctx = ExitStack()
    Q = Queues()
    with ctx:
        def sb(name, shape, dt=F32):
            return ctx.enter_context(nc.sbuf_tensor("s_" + name, shape, dt))

        def sem(name):
            return ctx.enter_context(nc.semaphore("m_" + name))

        def dram(name, shape, dt):
            return nc.dram_tensor("w_" + name, shape, dt, kind="Internal").ap()

        ident = sb("ident", [128, 128])
        wq = sb("wq", [128, 2, 256])
        wk = sb("wk", [128, 2, 256])
        wv = sb("wv", [128, 2, 256])
        wo = sb("wo", [128, 2, 256])
        bo = sb("bo", [128, 256])
        fq = sb("fq", [128, 2, 512])
        fk = sb("fk", [128, 2, 512])
        fg = sb("fg", [128, 2, 400])
        fo = sb("fo", [128, 3, 256])
        nhalf = sb("nhalf", [128, 4])
        xa = sb("xa", [128, 3, 4, 256])
        xt = sb("xt", [128, 2, 512])
        sta = sb("sta", [128, 4, 6])
        mva = sb("mva", [128, 4, 2])
        vea = sb("vea", [128, 4])
        rsa = sb("rsa", [128, 4])
        pt = sb("pt", [128, 3, 512], BF)
        qs = sb("qs", [128, 2, 8, 512], BF)
        ks = sb("ks", [128, 2, 8, 512], BF)
        v32 = sb("v32", [128, 4, 16, 17])
        mxa = sb("mxa", [128, 2, 4, 8])
        mp = sb("mp", [8, 1, 3, 512], BF)
        pa = sb("pa", [128, 6, 512])
        t1 = sb("t1", [128, 1, 512])
        xn = sb("xn", [128, 4, 256])
        rca = sb("rca", [128, 2, 16])
        comb = sb("comb", [128, 512])[:, :]
        ont = sb("ont", [128, 2, 512])
        stf = sb("stf", [128, 4, 6])
        mvf = sb("mvf", [128, 4, 2])
        vef = sb("vef", [128, 4])
        rsf = sb("rsf", [128, 4])
        nf = sb("nf", [128, 4, 256])
        prod = sb("prod", [128, 4, 2, 64])
        xf = sb("xf", [128, 2, 512])
        xg = sb("xg", [128, 4, 400])
        cmpt = sb("cmpt", [128, 64, 5, 5], mybir.dt.uint8)
        rank = sb("rank", [128, 64, 5])
        mask = sb("mask", [128, 2, 4, 2, 8, 5])
        sg = sb("sg", [128, 4, 8, 5])
        sg2 = sb("sg2", [128, 4, 8, 5])
        wvx = sb("wvx", [128, 4, 8, 5])
        vh = sb("vh", [128, 4, 8, 64])
        q1 = sb("q1", [128, 4, 512], F32R)
        q2 = sb("q2", [128, 4, 512], F32R)
        k1 = sb("k1", [128, 4, 512], F32R)
        k2 = sb("k2", [128, 4, 512], F32R)
        mxf = sb("mxf", [128, 2, 4, 2])
        mfh = sb("mfh", [2, 2, 512], F32R)
        pf = sb("pf", [128, 6, 512])
        acc = sb("acc", [128, 2, 512])
        osb = sb("osb", [128, 512])
        rcf = sb("rcf", [128, 2, 4])
        w2 = sb("w2", [128, 2, 4, 5])
        pu = sb("pu", [128, 2, 320])
        uu = sb("uu", [128, 4, 320])
        ut = sb("ut", [128, 3, 512])
        ots = sb("ots", [128, 4, 128])

        bank = [ctx.enter_context(nc.psum_tensor(f"bank{i}", [128, 512], F32)) for i in range(8)]

        parts = dram("parts", [2, 2, 2, 3, 128, 512], BF)
        maxa = dram("maxa", [2, 2, 3, 8, 512], BF)
        maxf = dram("maxf", [4, 2, 2, 512], F32)

        dma_sems, dma_counts = {}, {}

        def op(thread, eng, fn, deps=(), cost=0.3):
            return Q.add(thread, eng, fn, list(deps), cost)

        def pe(th, fn, deps=(), cost=0.22):
            return op(th, "tensor", fn, deps, cost)

        def act(th, fn, deps=(), cost=0.48):
            return op(th, "scalar", fn, deps, cost)

        def dve(th, fn, deps=(), cost=0.6):
            return op(th, "vector", fn, deps, cost)

        def pool(th, fn, deps=(), cost=1.0):
            return op(th, "gpsimd", fn, deps, cost)

        def dma(th, site, dst, src, deps=(), cost=2.5):
            if site not in dma_sems:
                dma_sems[site] = sem("d_" + site)
                dma_counts[site] = [0, None]
            last = dma_counts[site][1]
            s = Q.add(th, "sync", lambda e: e.dma_start(dst, src), list(deps) + [last], cost, dma=site)
            dma_counts[site][0] += 16
            dma_counts[site][1] = s
            s.sem, s.value = dma_sems[site], dma_counts[site][0]
            return s

        class Ring:

            def __init__(self, banks):
                self.banks, self.readers, self.n = banks, [[] for _ in banks], -1

            def take(self):
                self.n = (self.n + 1) % len(self.banks)
                return self.banks[self.n], self.readers[self.n], self.n

            def read_by(self, n, *steps):
                self.readers[n] = list(steps)

        rap = ram = Ring(bank[0:2])
        rae = Ring(bank[2:3])
        rff = rfm = Ring(bank[3:5])
        rfe = Ring(bank[5:6])
        oa, of = bank[6], bank[7]

        x0 = dma("ld", "x0", xa[:, 0, :, :], t["x"][0].rearrange("(c p) n -> p c n", p=128))
        loads = []
        for name, dst, src in [
            ("ident", ident[:, :], t["ident"]),
            ("wq", wq[:, :, :], t["wq"].rearrange("(c p) n -> p c n", p=128)),
            ("wk", wk[:, :, :], t["wk"].rearrange("(c p) n -> p c n", p=128)),
            ("wv", wv[:, :, :], t["wv"].rearrange("(c p) n -> p c n", p=128)),
            ("wo", wo[:, :, :], t["wo"].rearrange("(c p) n -> p c n", p=128)),
            ("bo", bo[:, :], t["bo"]),
            ("fq", fq[:, :, :], t["fq"].rearrange("(c p) n -> p c n", p=128)),
            ("fk", fk[:, :, :], t["fk"].rearrange("(c p) n -> p c n", p=128)),
            ("fg", fg[:, :, :], t["fg"].rearrange("(c p) n -> p c n", p=128)),
            ("fo", fo[:, 0:2, :], t["fo"][0:256, :].rearrange("(c p) n -> p c n", p=128)),
            ("fo2", fo[0:64, 2, :], t["fo"][256:320, :]),
        ]:
            loads.append(dma("ld", name, dst, src))
        L = dict(zip(["ident", "wq", "wk", "wv", "wo", "bo", "fq", "fk", "fg", "fo", "fo2"], loads))
        c_half = pool("c", lambda e: e.memset(nhalf[:, :], -0.5))
        c_v32 = pool("c", lambda e: e.memset(v32[:, :, :, 16:17], 1.0))
        c_oa = dve("c", lambda e: e.memset(oa[:, :], 0.0))
        for c in range(2):
            for u in range(4):
                c_ks = dve("c", lambda e, c=c, u=u: e.memset(ks[96:99, c, 2 * u:2 * u + 2, :], 1.0), cost=1.07)
        c_k2z = dve("c", lambda e: e.memset(k2[64:128, :, :].bitcast(F32), 0.0))
        c_k2o = dve("c", lambda e: e.memset(k2[64:66, :, :].bitcast(F32), 1.0), [c_k2z])
        c_q2z = dve("c", lambda e: e.memset(q2[64:128, :, :].bitcast(F32), 0.0))
        c_cmp = dve("c", lambda e: e.memset(cmpt[:, :, :, :], 0.0))

        def layernorm(th, x, st, mv, ve, rs, out, ready, free):
            a = [dve(th, lambda e, i=i: e.bn_stats(st[:, i, :], x[:, i, :]), [ready], 0.35) for i in range(4)]
            g = [dve(th, lambda e, i=i: e.bn_aggr(mv[:, i, :], st[:, i, :]), [a[i]], 0.12) for i in range(4)]
            v = dve(th, lambda e: e.tensor_scalar_add(ve[:, :], mv[:, :, 1], 1e-5), [g[3]], 0.1)
            r = pool(th, lambda e: e.tensor_tensor(rs[:, :], ve[:, :], nhalf[:, :], ALU.pow), [v, c_half], 1.0)
            return [dve(th, lambda e, i=i: e.tensor_scalar(out[:, i, :], x[:, i, :], mv[:, i, 0:1], rs[:, i:i + 1],
                                                          ALU.subtract, ALU.mult), [r] + free, 0.32)
                    for i in range(4)]

        def transposed(th, ring, src, dst, ready, free):
            out = []
            for f in range(2):
                b, busy, n = ring.take()

                def go(e, b=b, f=f):
                    for i in range(4):
                        r = e.transpose(b[:, 128 * i:128 * i + 128], src[:, i, 128 * f:128 * f + 128], ident[:, :])
                    return r
                p = pe(th, go, busy + ready + [L["ident"]], 0.5)
                c = act(th, lambda e, b=b, f=f: e.copy(dst[:, f, :], b[:, :]), [p] + free)
                ring.read_by(n, c)
                out.append((p, c))
            return [p for p, _ in out], [c for _, c in out]

        def attn(b, S):
            A, X = b % 2, b % 3
            x = xa[:, X, :, :]
            ld = x0 if b == 0 else dma("ld", f"x{X}", x, t["x"][b].rearrange("(c p) n -> p c n", p=128), [S["xfree"][X]])
            nrm = layernorm("ap", x, sta, mva, vea, rsa, xn, ld, [S["xn"]])
            xb = [pool("ap", lambda e, i=i: e.tensor_tensor(x[:, i, :], x[:, i, :], bo[:, :], ALU.add),
                       [nrm[3], L["bo"]], 0.7) for i in range(4)]
            tp, tc_ = transposed("ap", rap, xn, xt, nrm, S["xt"])
            S["xn"] = tp[1]
            stacked, rows, proj = {}, [], []
            for c in range(2):
                for z, (w, lw, dst) in enumerate(((wq, "wq", qs), (wk, "wk", ks))):
                    bk, busy, n = rap.take()

                    def go(e, bk=bk, w=w, c=c):
                        for f in range(2):
                            r = e.matmul(bk[:, :], w[:, f, 128 * c:128 * c + 128], xt[:, f, :],
                                         start=(f == 0), stop=(f == 1))
                        return r
                    p = pe("ap", go, busy + tc_ + [L[lw]], 1.72)
                    proj.append(p)
                    hi = act("ap", lambda e, bk=bk: e.copy(pt[:, 0, :], bk[:, :]), [p, S["pt"]])
                    r1 = dve("ap", lambda e, bk=bk: e.tensor_tensor(bk[:, :], bk[:, :], pt[:, 0, :], ALU.subtract), [hi])
                    mid = act("ap", lambda e, bk=bk: e.copy(pt[:, 1, :], bk[:, :]), [r1])
                    lo = dve("ap", lambda e, bk=bk: e.tensor_tensor(pt[:, 2, :], bk[:, :], pt[:, 1, :], ALU.subtract),
                             [mid])
                    rap.read_by(n, lo)
                    st = dma("ap", f"pw{z}{c}", parts[A, z, c].rearrange("s p n -> p s n"), pt[:, :, :],
                             [lo] + S["parts"][A, z, c])
                    S["pt"] = st
                    sd = parts[A, z, c].rearrange("s (d h) n -> (s d) h n", h=8)
                    cuts = [(0, 0, 48), (48, 0, 32), (80, 0, 16)] if z == 0 else \
                        [(0, 0, 16), (16, 0, 16), (32, 0, 16), (48, 16, 16), (64, 16, 16), (80, 32, 16)]
                    for u in range(2):
                        stacked[z, c, u] = [dma("ap", f"pr{z}{c}{j}{u}", dst[to:to + k, c, 4 * u:4 * u + 4, :],
                                                sd[fr:fr + k, 4 * u:4 * u + 4, :], [st] + S["stack"][c, u])
                                            for j, (to, fr, k) in enumerate(cuts)]
                    S["parts"][A, z, c] = stacked[z, c, 0] + stacked[z, c, 1]
                for h in range(8):
                    for i in range(4):
                        bk, busy, n = ram.take()
                        p = pe("am", lambda e, bk=bk, c=c, h=h, i=i: e.matmul(
                            bk[:, :], qs[0:96, c, h, 128 * i:128 * i + 128], ks[0:96, c, h, :], start=True, stop=True),
                            busy + stacked[0, c, h // 4] + stacked[1, c, h // 4])
                        mx = dve("am", lambda e, bk=bk, c=c, h=h, i=i: e.tensor_reduce(
                            mxa[:, c, i, h:h + 1], bk[:, :], AX.X, ALU.max, negate=True), [p, S["mxa"][c]])
                        ram.read_by(n, mx)
                bk, busy, n = ram.take()

                def go(e, bk=bk, c=c):
                    for i in range(4):
                        r = e.transpose(bk[0:8, 128 * i:128 * i + 128], mxa[:, c, i, :], ident[:, :])
                    return r
                p = pe("am", go, busy + [mx], 0.45)
                S["mxa"][c] = p
                h1 = act("am", lambda e, bk=bk: e.copy(mp[:, 0, 0, :], bk[0:8, :]), [p, S["mp"]])
                r1 = dve("am", lambda e, bk=bk: e.tensor_tensor(bk[0:8, :], bk[0:8, :], mp[:, 0, 0, :], ALU.subtract), [h1])
                m1 = act("am", lambda e, bk=bk: e.copy(mp[:, 0, 1, :], bk[0:8, :]), [r1])
                l1 = dve("am", lambda e, bk=bk: e.tensor_tensor(mp[:, 0, 2, :], bk[0:8, :], mp[:, 0, 1, :], ALU.subtract),
                         [m1])
                ram.read_by(n, l1)
                w = dma("am", f"mw{c}", maxa[A, c].rearrange("s h n -> h s n"), mp[:, 0, :, :], [l1, S["maxa"][A, c]])
                S["mp"] = w
                g = dma("am", f"mr{c}", qs[96:99, c, :, :], maxa[A, c], [w] + S["stack"][c, 0] + S["stack"][c, 1])
                S["maxa"][A, c] = g
                rows.append(g)
            vd = []
            for i2 in range(2):
                bk, busy, n = rae.take()

                def go(e, bk=bk, i2=i2):
                    for i in range(2):
                        for f in range(2):
                            tc = 2 * i2 + i
                            r = e.matmul(bk[:, 256 * i:256 * i + 256], xt[:, f, 128 * tc:128 * tc + 128], wv[:, f, :],
                                         start=(f == 0), stop=(f == 1))
                    return r
                p = pe("av", go, busy + tc_ + [L["wv"]], 1.74)
                c_ = act("av", lambda e, bk=bk, i2=i2: e.copy(
                    v32[:, 2 * i2:2 * i2 + 2, :, 0:16], bk[:, :].rearrange("p (i h d) -> p i h d", i=2, h=16)),
                    [p, c_v32, S["v32"]])
                rae.read_by(n, c_)
                vd.append(c_)
            S["xt"] = [p, proj[-1]]
            outs = []
            for j in range(4):
                c = j // 2
                for kc in range(4):
                    ex, slots = [], []
                    for g in range(4):
                        h = 4 * (j % 2) + g
                        S["pn"] = (S["pn"] + 1) % 6
                        slot = S["pn"]
                        slots.append(slot)
                        bk, busy, n = rae.take()
                        p = pe("ae", lambda e, bk=bk, c=c, h=h, kc=kc: e.matmul(
                            bk[:, :], ks[0:99, c, h, 128 * kc:128 * kc + 128], qs[0:99, c, h, :],
                            start=True, stop=True), busy + [rows[c], c_ks])
                        x_ = act("ae", lambda e, bk=bk, slot=slot: e.activation(
                            pa[:, slot, :], bk[:, :], ACT.Exp, scale=0.0625), [p, S["pa"][slot]], 0.48)
                        rae.read_by(n, x_)
                        ex.append(x_)

                    def go(e, slots=tuple(slots), kc=kc, j=j):
                        for g in range(4):
                            r = e.matmul(oa[32 * g:32 * g + 17, :], v32[:, kc, 4 * j + g, :], pa[:, slots[g], :],
                                         start=(kc == 0), stop=(kc == 3))
                        return r
                    pv = pe("apv", go, ex + vd + ([S["oa"], c_oa] if kc == 0 else []), 0.98)
                    for slot in slots:
                        S["pa"][slot] = pv
                S["stack"][c, j % 2] = [p]
                B, a = 0, j % 2
                tr = dve("apv", lambda e, B=B: e.transpose(t1[:, B, :], oa[:, :]), [pv, S["t1"][B]])
                S["oa"] = tr
                t4 = t1[:, B, :].rearrange("p (k j) -> p k j", j=32)
                rc = dve("apv", lambda e, B=B, t4=t4: e.reciprocal(rca[:, B, :], t4[:, :, 16]), [tr], 0.15)
                ml = dve("apv", lambda e, B=B, t4=t4, a=a: e.tensor_tensor(
                    comb.rearrange("p (k j) -> p k j", j=32)[:, :, 16 * a:16 * a + 16], t4[:, :, 0:16],
                    rca[:, B, :].unsqueeze(2).to_broadcast([128, 16, 16]), ALU.mult), [rc, S["comb"]], 0.35)
                S["t1"][B] = ml
                if a:
                    tt = dve("apv", lambda e, j=j: e.transpose(ont[:, j // 2, :], comb), [ml, S["ont"]])
                    S["comb"] = tt
                    outs.append(tt)
            S["v32"] = pv
            for i2 in range(2):
                bk, busy, n = rae.take()

                def go(e, bk=bk, i2=i2):
                    for i in range(2):
                        for f in range(2):
                            tc = 2 * i2 + i
                            r = e.matmul(bk[:, 256 * i:256 * i + 256], ont[:, f, 128 * tc:128 * tc + 128], wo[:, f, :],
                                         start=(f == 0), stop=(f == 1))
                    return r
                p = pe("ae", go, busy + outs + [L["wo"]], 1.74)
                s = dve("ae", lambda e, bk=bk, i2=i2: e.tensor_tensor(
                    x[:, 2 * i2:2 * i2 + 2, :], bk[:, :].rearrange("p (i n) -> p i n", i=2),
                    x[:, 2 * i2:2 * i2 + 2, :], ALU.add), [p, xb[3]])
                rae.read_by(n, s)
            S["ont"] = p
            return s

        def moe(b, ready, S):
            M, X = b % 2, b % 3
            x = xa[:, X, :, :]
            nrm = layernorm("fq", x, stf, mvf, vef, rsf, nf, ready, [S["nf"]])
            tp, tc_ = transposed("fq", rff, nf, xf, nrm, S["xf"])
            S["nf"] = tp[1]
            gc = []
            for i in range(4):
                bk, busy, n = rff.take()

                def go(e, bk=bk, i=i):
                    for f in range(2):
                        r = e.matmul(bk[:, 0:400], xf[:, f, 128 * i:128 * i + 128], fg[:, f, :],
                                     start=(f == 0), stop=(f == 1))
                    return r
                p = pe("fq", go, busy + tc_ + [L["fg"]], 1.36)
                c_ = act("fq", lambda e, bk=bk, i=i: e.copy(xg[:, i, :], bk[:, 0:400]), [p, S["xg"], S["cm"]], 0.4)
                rff.read_by(n, c_)
                gc.append(c_)
            gl = xg[:, :, 320:400].rearrange("p i (g e) -> p i g e", e=5)
            cm = cmpt[:, :, :, :].rearrange("p (i g) a c -> p i g a c", i=4)
            prev = []
            for e_ in range(5):
                if e_ < 4:
                    prev.append(dve("fq", lambda e, e_=e_: e.tensor_tensor(
                        cm[:, :, :, e_ + 1:5, e_], gl[:, :, :, e_:e_ + 1].to_broadcast([128, 4, 16, 4 - e_]),
                        gl[:, :, :, e_ + 1:5], ALU.is_ge), gc + [c_cmp, S["cm"]], 0.07 * (5 - e_)))
                if e_ > 0:
                    prev.append(dve("fq", lambda e, e_=e_: e.tensor_tensor(
                        cm[:, :, :, 0:e_, e_], gl[:, :, :, e_:e_ + 1].to_broadcast([128, 4, 16, e_]),
                        gl[:, :, :, 0:e_], ALU.is_gt), gc + [c_cmp, S["cm"]], 0.07 * (e_ + 1)))
            rk = dve("fq", lambda e: e.tensor_reduce(rank[:, :, :], cmpt[:, :, :, :], AX.X, ALU.add), [prev[-1]], 1.74)
            S["cm"] = rk
            mk = dve("fq", lambda e: e.tensor_scalar(mask[:, M, :, :, :, :].rearrange("p i z h e -> p (i z h e)"),
                                                     rank[:, :, :].rearrange("p g e -> p (g e)"), 1.5, None,
                                                     ALU.is_lt), [rk, S["mask"][M]], 0.3)
            e1 = act("fq", lambda e: e.activation(sg[:, :, :, :].rearrange("p i h e -> p i (h e)"),
                                                  xg[:, :, 320:360], ACT.Exp, scale=-1.0), [gc[3], S["sg"]], 0.23)
            s1 = dve("fq", lambda e: e.tensor_scalar_add(sg2[:, :, :, :], sg[:, :, :, :], 1.0), [e1], 0.2)
            s2 = dve("fq", lambda e: e.reciprocal(sg[:, :, :, :], sg2[:, :, :, :]), [s1], 1.07)
            s3 = dve("fq", lambda e: e.tensor_tensor(wvx[:, :, :, :], sg[:, :, :, :], mask[:, M, :, 0, :, :], ALU.mult),
                     [s2, mk, S["wvx"]], 0.25)
            S["sg"] = s3
            qk = {}

            def front(pair):
                qd = []
                for z in range(2):
                    w, lw = ((fq, "fq"), (fk, "fk"))[z]
                    bk, busy, n = rff.take()
                    col = 128 * pair

                    def go(e, bk=bk, w=w, col=col):
                        for f in range(2):
                            r = e.matmul(bk[:, :], w[:, f, col:col + 128], xf[:, f, :], start=(f == 0), stop=(f == 1))
                        return r
                    p = pe("fq", go, busy + tc_ + [L[lw]], 1.72)
                    S["proj"] = p
                    a_ = []
                    for u in range(2):
                        s = 2 * (pair % 2) + u
                        src = bk[64 * u:64 * u + 64, :]
                        free = S["stk"][s]
                        up, dn = ((q1[0:64, s, :], q2[0:64, s, :]), (k1[0:64, s, :], k1[64:128, s, :]))[z]
                        a1 = act("fq", lambda e, up=up, src=src: e.copy(up, src), [p] + free, 0.48)
                        a2 = act("fq", lambda e, dn=dn, src=src: e.copy(dn, src), [p, c_q2z] + free, 0.48)
                        a_ += [a1, a2]
                    for u in range(2):
                        s = 2 * (pair % 2) + u
                        src = bk[64 * u:64 * u + 64, :]
                        up, to = ((q1[0:64, s, :], q1[64:128, s, :]), (k1[0:64, s, :], k2[0:64, s, :]))[z]
                        d1 = dve("fq", lambda e, up=up, src=src, to=to: e.tensor_tensor(
                            to, src, up.bitcast(F32), ALU.subtract), a_ + S["stk"][s])
                        qd += [d1]
                    rff.read_by(n, d1)
                    qd += a_
                B = pair % 2
                for u in range(2):
                    s = 2 * B + u
                    for i in range(4):
                        bk, busy, n = rfm.take()
                        p = pe("fm", lambda e, bk=bk, s=s, i=i: e.matmul(
                            bk[:, :], q1[:, s, 128 * i:128 * i + 128], k1[:, s, :], start=True, stop=True), busy + qd)
                        mx = dve("fm", lambda e, bk=bk, B=B, u=u, i=i: e.tensor_reduce(
                            mxf[:, B, i, u:u + 1], bk[:, :], AX.X, ALU.max, negate=True), [p, S["mxf"][B]])
                        rfm.read_by(n, mx)
                bk, busy, n = rfm.take()

                def go(e, bk=bk):
                    for i in range(4):
                        r = e.transpose(bk[0:2, 128 * i:128 * i + 128], mxf[:, B, i, :], ident[:, :])
                    return r
                p = pe("fm", go, busy + [mx], 0.43)
                S["mxf"][B] = p
                h1 = act("fm", lambda e, bk=bk: e.copy(mfh[:, 0, :], bk[0:2, :]), [p, S["mfh"]])
                l1 = dve("fm", lambda e, bk=bk: e.tensor_tensor(mfh[:, 1, :], bk[0:2, :], mfh[:, 0, :].bitcast(F32),
                                                                ALU.subtract), [h1])
                rfm.read_by(n, l1)
                w = dma("fm", f"fw{pair}", maxf[pair].rearrange("s h n -> h s n"), mfh[:, :, :].bitcast(F32),
                        [l1, S["maxf"][pair]])
                S["mfh"] = w
                row = dma("fm", f"fr{pair}", q2[64:66, 2 * B:2 * B + 2, :].bitcast(F32), maxf[pair],
                          [w, c_q2z] + S["stk"][2 * B] + S["stk"][2 * B + 1])
                S["maxf"][pair] = row
                qk[pair] = qd + [row]

            def values(pair):
                last = None
                for e_ in range(5):
                    to = vh[:, :, 2 * pair:2 * pair + 2, 0:64] if e_ == 0 else prod[:, :, :, :]
                    xv = xg[:, :, 64 * e_:64 * e_ + 64]
                    m = pool("fv", lambda e, to=to, xv=xv, e_=e_: e.tensor_tensor(
                        to, xv.unsqueeze(2).to_broadcast([128, 4, 2, 64]),
                        wvx[:, :, 2 * pair:2 * pair + 2, e_:e_ + 1].to_broadcast([128, 4, 2, 64]), ALU.mult),
                        [s3] + gc + [S["v65"][pair] if e_ == 0 else last], 1.0)
                    if e_ == 0:
                        last = m
                    else:
                        vv = vh[:, :, 2 * pair:2 * pair + 2, 0:64]
                        last = pool("fv", lambda e, vv=vv: e.tensor_tensor(vv, vv, prod[:, :, :, :], ALU.add), [m], 1.22)
                return last

            def heads(pair, vm):
                adds = [None, None]
                for kc in range(4):
                    ex, slots = [], []
                    for u in range(2):
                        s = 2 * (pair % 2) + u
                        bk, busy, n = rfe.take()
                        S["pn"] = ps = (S["pn"] + 1) % 6
                        slots.append(ps)

                        def go(e, bk=bk, s=s, kc=kc):
                            e.matmul(bk[:, :], k1[:, s, 128 * kc:128 * kc + 128], q1[:, s, :], start=True, stop=False)
                            return e.matmul(bk[:, :], k2[:, s, 128 * kc:128 * kc + 128], q2[:, s, :],
                                            start=False, stop=True)
                        p = pe("fe", go, busy + qk[pair] + [c_k2o], 0.44)
                        x_ = act("fe", lambda e, bk=bk, ps=ps: e.activation(pf[:, ps, :], bk[:, :], ACT.Exp,
                                                                            scale=0.125), [p] + S["pf"][ps], 0.48)
                        rfe.read_by(n, x_)
                        ex.append(x_)
                        S["stk"][s] = [p]

                    def go(e, slots=tuple(slots), kc=kc):
                        for u in range(2):
                            r = e.matmul(of[64 * u:64 * u + 64, :], vh[:, kc, 2 * pair + u, :], pf[:, slots[u], :],
                                         start=(kc == 0), stop=(kc == 3))
                        return r
                    pv = pe("fpv", go, ex + [vm] + ([S["of"]] if kc == 0 else []), 0.91)
                    for u in range(2):
                        if kc == 0:
                            S["pf"][slots[u]] = [pv]
                            continue
                        was = pf[:, prev[u], :] if kc == 1 else acc[:, u, :]
                        adds[u] = pool("fs", lambda e, u=u, was=was, ps=slots[u]: e.tensor_tensor(
                            acc[:, u, :], was, pf[:, ps, :], ALU.add),
                            [ex[u]] + ([ex0[u], S["acc"][u]] if kc == 1 else [adds[u]]), 1.1)
                        S["pf"][slots[u]] = [pv, adds[u]]
                        if kc == 1:
                            S["pf"][prev[u]] = S["pf"][prev[u]] + [adds[u]]
                    prev, ex0 = slots, ex
                S["v65"][pair] = pv
                ev = act("fpv", lambda e: e.copy(osb[:, :], of[:, :]), [pv, S["osb"]], 0.48)
                busy, rcs = ev, []
                for u in range(2):
                    def go(e, u=u):
                        for i in range(4):
                            r = e.transpose(of[:, 128 * i:128 * i + 128], acc[:, u, 128 * i:128 * i + 128], ident[:, :])
                        return r
                    S["acc"][u] = tr = pe("fpv", go, [busy, adds[u]], 0.24)
                    busy = sr = dve("fpv", lambda e, u=u: e.tensor_reduce(
                        rcf[:, u, :], of[:, :].rearrange("p (i k) -> p i k", k=128), AX.X, ALU.add), [tr, S["rcf"]], 0.6)

                def go(e):
                    for i in range(4):
                        r = e.transpose(of[:, 128 * i:128 * i + 128], osb[:, 128 * i:128 * i + 128], ident[:, :])
                    return r
                S["osb"] = tr = pe("fpv", go, [busy, ev], 0.24)
                S["of"] = oc = act("fpv", lambda e: e.copy(ots[:, :, :], of[:, :].rearrange("p (i d) -> p i d", d=128)),
                                   [tr, S["ots"]], 0.48)
                rc = dve("fpv", lambda e: e.reciprocal(rcf[:, :, :], rcf[:, :, :]), [sr], 0.15)
                for u in range(2):
                    h = 2 * pair + u
                    ww = dve("fpv", lambda e, u=u, h=h: e.tensor_tensor(
                        w2[:, u, :, :], mask[:, M, :, 1, h, :], rcf[:, u, :].unsqueeze(2).to_broadcast([128, 4, 5]),
                        ALU.mult), [rc, mk, S["w2"][u]], 0.09)
                    for i2 in range(2):
                        first = h == 0
                        cut = slice(2 * i2, 2 * i2 + 2)
                        to = uu[:, cut, :] if first else pu[:, :, :]
                        um = pool("fpv", lambda e, u=u, to=to, cut=cut: e.tensor_tensor(
                            to.rearrange("p i (e k) -> p i e k", k=64),
                            ots[:, cut, 64 * u:64 * u + 64].unsqueeze(2).to_broadcast([128, 2, 5, 64]),
                            w2[:, u, cut, :].unsqueeze(3).to_broadcast([128, 2, 5, 64]), ALU.mult),
                            [ww, oc, S["uu"] if first else S["ua"][1]], 1.22)
                        if first:
                            S["ua"][i2] = um
                        else:
                            S["ua"][i2] = pool("fpv", lambda e, cut=cut: e.tensor_tensor(
                                uu[:, cut, :], uu[:, cut, :], pu[:, :, :], ALU.add), [um, S["ua"][i2]], 1.5)
                            S["ua"][1] = S["ua"][i2]
                    S["w2"][u] = um
                S["ots"] = um
                S["mask"][M] = S["rcf"] = ww

            vals = []
            for pair in range(4):
                front(pair)
                vals.append(values(pair))
                heads(pair, vals[pair])
            S["xg"] = S["wvx"] = vals[3]
            S["xf"] = [S["proj"]]
            uc = []
            for k3, m in enumerate((128, 128, 64)):
                bk, busy, n = rfe.take()

                def go(e, bk=bk, k3=k3, m=m):
                    for i in range(4):
                        r = e.transpose(bk[0:m, 128 * i:128 * i + 128], uu[:, i, 128 * k3:128 * k3 + m], ident[:, :])
                    return r
                p = pe("fe", go, busy + S["ua"], 0.48)
                c_ = act("fe", lambda e, bk=bk, k3=k3, m=m: e.copy(ut[0:m, k3, :], bk[0:m, :]), [p, S["ut"]], 0.48)
                rfe.read_by(n, c_)
                uc.append(c_)
            S["uu"] = p
            for i2 in range(2):
                bk, busy, n = rfe.take()

                def go(e, bk=bk, i2=i2):
                    for i in range(2):
                        tc = 2 * i2 + i
                        for k3, m in enumerate((128, 128, 64)):
                            r = e.matmul(bk[:, 256 * i:256 * i + 256], ut[0:m, k3, 128 * tc:128 * tc + 128],
                                         fo[0:m, k3, :], start=(k3 == 0), stop=(k3 == 2))
                    return r
                p = pe("fe", go, busy + uc + [L["fo"], L["fo2"]], 2.6)
                s = dve("fe", lambda e, bk=bk, i2=i2: e.tensor_tensor(
                    x[:, 2 * i2:2 * i2 + 2, :], bk[:, :].rearrange("p (i n) -> p i n", i=2),
                    x[:, 2 * i2:2 * i2 + 2, :], ALU.add), [p])
                rfe.read_by(n, s)
            S["ut"] = p
            return dma("st", f"out{X}", t["out"][b].rearrange("(c p) n -> p c n", p=128), x, [s])

        SA = {"xfree": [None] * 3, "xn": None, "xt": [], "pt": None, "stack": {(c, u): [] for c in range(2) for u in range(2)}, "v32": None,
              "parts": {(a, z, c): [] for a in range(2) for z in range(2) for c in range(2)},
              "mxa": [None, None], "mp": None, "maxa": {(a, c): None for a in range(2) for c in range(2)},
              "pa": [None] * 6, "pn": 0, "oa": None, "t1": [None, None], "comb": None, "ont": None}
        SF = {"nf": None, "xf": [], "xg": None, "cm": None, "mask": [None] * 2, "sg": None, "wvx": None,
              "v65": [None] * 4, "stk": [[] for _ in range(4)], "mxf": [None] * 2, "mfh": None, "maxf": [None] * 4,
              "pf": [[] for _ in range(6)], "pn": 0, "acc": [None] * 2, "rcf": None, "w2": [None] * 2, "of": None, "osb": None, "ots": None, "pu": [None] * 2, "ua": [None] * 4, "uu": None, "ut": None}
        for b in range(t["nb"]):
            r = attn(b, SA)
            o = moe(b, r, SF)
            SA["xfree"][b % 3] = o

        Q.settle({
            "sync": (0.00, "am ap fm ld st".split()),
            "tensor": (0.05, "ae ap am fm fe apv av fpv fq".split()),
            "scalar": (0.10, "av ae fm am fpv ap fe fq".split()),
            "vector": (0.00, "fq fm fe apv ae fpv am ap c".split()),
            "gpsimd": (0.00, "fs ap fpv fv fq c".split()),
        })
        eng_sem = {e: sem("e_" + e) for e in ENGINES}
        for e in ENGINES:
            n = 0
            for s in Q.order[e]:
                if s.dma is None and s.used:
                    n += 1
                    s.sem, s.value = eng_sem[e], n
        final = [(dma_sems[k], dma_counts[k][0]) for k in dma_counts]

        def emit(name):
            def body(e):
                seen = {}
                for s in Q.order[name]:
                    need = {}
                    for d in s.deps:
                        k = id(d.sem)
                        if seen.get(k, 0) < d.value and need.get(k, (None, 0))[1] < d.value:
                            need[k] = (d.sem, d.value)
                    for k, (m, v) in need.items():
                        e.wait_ge(m, v)
                        seen[k] = v
                    r = s.fn(e)
                    if s.dma is not None:
                        r.then_inc(s.sem, 16)
                    elif s.used:
                        r.then_inc(s.sem, 1)
                if name == "sync":
                    for m, v in final:
                        e.wait_ge(m, v)
            return body

        block = ctx.enter_context(nc.Block())
        block.sync(emit("sync"))
        block.tensor(emit("tensor"))
        block.scalar(emit("scalar"))
        block.vector(emit("vector"))
        block.gpsimd(emit("gpsimd"))


def kernel(L0_attn_x, L0_attn_Wk, L0_attn_Wq, L0_attn_Wv, L0_attn_Wo, L0_attn_bo, L0_ffn_Wq, L0_ffn_Wk, L0_ffn_Ws,
           L0_ffn_Wd, L0_ffn_Wv, L0_ffn_Wo):
    import concourse.bacc as bacc
    from concourse.bass_utils import run_bass_kernel_spmd

    def qk(w):
        return np.asarray(w).T.reshape(256, 2, 8, 16).transpose(0, 1, 3, 2).reshape(256, 256)

    arrays = {
        "x": np.asarray(L0_attn_x),
        "wq": qk(L0_attn_Wq),
        "wk": qk(L0_attn_Wk),
        "wv": np.asarray(L0_attn_Wv).T,
        "wo": np.asarray(L0_attn_Wo).T.reshape(2, 2, 4, 16, 256).transpose(0, 2, 1, 3, 4).reshape(256, 256),
        "bo": np.broadcast_to(np.asarray(L0_attn_bo), (128, 256)),
        "fq": np.asarray(L0_ffn_Wq),
        "fk": np.asarray(L0_ffn_Wk),
        "fg": np.concatenate([np.asarray(L0_ffn_Wv).transpose(1, 0, 2).reshape(256, 320), np.asarray(L0_ffn_Ws),
                              np.asarray(L0_ffn_Wd)], axis=1),
        "fo": np.asarray(L0_ffn_Wo).reshape(320, 256),
        "ident": np.eye(128, dtype=np.float32),
    }
    arrays = {k: np.ascontiguousarray(v) for k, v in arrays.items()}
    nb = arrays["x"].shape[0]
    nc = bacc.Bacc("TRN2", target_bir_lowering=False, num_devices=1)
    t = {k: nc.dram_tensor("in_" + k, v.shape, mybir.dt.from_np(v.dtype), kind="ExternalInput").ap()
         for k, v in arrays.items()}
    t["out"] = nc.dram_tensor("out_y", (nb, T, D), mybir.dt.float32, kind="ExternalOutput").ap()
    t["nb"] = nb
    program(nc, t)
    r = run_bass_kernel_spmd(nc, [{"in_" + k: v for k, v in arrays.items()}], core_ids=[0])
    return r.results[0]["out_y"]
```
